# Optimizing a Trainium2 kernel written in Bass

```python
import numpy as np
import jax
import jax.numpy as jnp

def _softmax(x, axis=-1):
    return jax.nn.softmax(x, axis=axis)

def _gelu(x):
    return jax.nn.gelu(x, approximate=True)

def _silu(x):
    return jax.nn.silu(x)

def _sigmoid(x):
    return jax.nn.sigmoid(x)

def _layernorm(x, axis=-1, eps=1e-05):
    m = jnp.mean(x, axis=axis, keepdims=True)
    v = jnp.var(x, axis=axis, keepdims=True)
    return (x - m) / jnp.sqrt(v + eps)

def _scatter_add(tgt, idx, src, axis=0):
    return tgt.at[idx].add(src)

def _segment_sum(src, seg, n):
    return jax.ops.segment_sum(src, seg, n)
kernel_name = 'mk_gnn_resnorm_d4_gnn_r8_11df9a'

def setup_inputs(seed: int=0):
    np.random.seed(seed)
    _w = jnp.asarray

    def _rec_inputs():
        import jax
        import jax.numpy as jnp
        _gk = jax.random.key(seed)
        x = -1.01e-05 + 0.05001 * jax.random.normal(jax.random.fold_in(_gk, 1), (6250, 64), jnp.float32)
        _s = jax.random.randint(jax.random.fold_in(_gk, 2), (100000,), 0, 6250, jnp.int32)
        _d = jax.random.randint(jax.random.fold_in(_gk, 3), (100000,), 0, 6250, jnp.int32)
        _loop = jnp.arange(6250, dtype=jnp.int32)
        src = jnp.concatenate([_s, _d, _loop])
        dst = jnp.concatenate([_d, _s, _loop])
        _o = jnp.argsort(dst, stable=True)
        src = src[_o]
        dst = dst[_o]
        edge_attr_64 = 9.41057e-06 + 1 * jax.random.normal(jax.random.fold_in(_gk, 12), (206250, 64), jnp.float32)
        node_vec1 = jax.random.uniform(jax.random.fold_in(_gk, 14), (6250, 1), jnp.float32, 0.0, 0.999993)
        node_vec1_n2 = jax.random.uniform(jax.random.fold_in(_gk, 15), (6250, 1), jnp.float32, 0.0, 0.999993)
        return (x, src, dst, edge_attr_64, node_vec1, node_vec1_n2)
    x, src, dst, edge_attr_64, node_vec1, node_vec1_n2 = _rec_inputs()

    def _L0_gnn_setup():
        import jax, jax.numpy as jnp
        import numpy as np
        N = 12500
        E = 400000
        D = 64
        key = jax.random.key(seed)
        k = jax.random.split(key, 7)
        weight = jax.random.normal(k[0], (N, D), dtype=jnp.float32) * 0.05
        ps_w = jax.random.normal(k[1], (1, D), dtype=jnp.float32) * 0.1
        review_feat = jax.random.normal(k[2], (E, D), dtype=jnp.float32)
        cj = jax.random.uniform(k[3], (N, 1), dtype=jnp.float32)
        ci = jax.random.uniform(k[4], (N, 1), dtype=jnp.float32)
        src = jax.random.randint(k[5], (E,), 0, N, dtype=jnp.int32)
        dst = jax.random.randint(k[6], (E,), 0, N, dtype=jnp.int32)
        return {'weight': weight, 'ps_w': ps_w, 'review_feat': review_feat, 'cj': cj, 'ci': ci, 'src': src, 'dst': dst}
    _L0_gnn_all = _L0_gnn_setup()
    _L0_gnn_in = {k: v for k, v in _L0_gnn_all.items() if k in ('ps_w',)}
    del _L0_gnn_all

    def _L1_gnn_setup():
        import jax, jax.numpy as jnp
        import numpy as np
        N_NODES = 12500
        N_EDGES = 156250
        D_IN, D_HID, D_OUT = (64, 64, 64)

        def _sage_conv(x, edge_index, W_l, b_l, W_r, num_nodes):
            src, dst = (edge_index[0], edge_index[1])
            msgs = x[src]
            agg = jax.ops.segment_sum(msgs, dst, num_segments=num_nodes)
            cnt = jax.ops.segment_sum(jnp.ones((src.shape[0],), x.dtype), dst, num_segments=num_nodes)
            mean = agg / jnp.maximum(cnt, 1.0)[:, None]
            return mean @ W_l.T + b_l + x @ W_r.T
        key = jax.random.key(seed)
        ks = jax.random.split(key, 8)
        s_in = 1.0 / np.sqrt(D_IN)
        s_hid = 1.0 / np.sqrt(D_HID)
        return {'x': jax.random.normal(ks[0], (N_NODES, D_IN), jnp.float32), 'edge_index': jax.random.randint(ks[1], (2, N_EDGES), 0, N_NODES, jnp.int32), 'W1_l': jax.random.normal(ks[2], (D_HID, D_IN), jnp.float32) * s_in, 'b1': jnp.zeros((D_HID,), jnp.float32), 'W1_r': jax.random.normal(ks[3], (D_HID, D_IN), jnp.float32) * s_in, 'W2_l': jax.random.normal(ks[4], (D_OUT, D_HID), jnp.float32) * s_hid, 'b2': jnp.zeros((D_OUT,), jnp.float32), 'W2_r': jax.random.normal(ks[5], (D_OUT, D_HID), jnp.float32) * s_hid}
    _L1_gnn_all = _L1_gnn_setup()
    _L1_gnn_in = {k: v for k, v in _L1_gnn_all.items() if k in ('W1_l', 'b1', 'W1_r', 'W2_l', 'b2', 'W2_r')}
    del _L1_gnn_all

    def _L2_gnn_setup():
        import jax, jax.numpy as jnp
        import numpy as np
        N = 12500
        E = 200000
        D_IN = 64
        D_OUT = 64
        ALPHA = 0.5

        def _mean_agg(feat_src, idx_dst, num_nodes):
            summed = jax.ops.segment_sum(feat_src, idx_dst, num_segments=num_nodes)
            cnt = jax.ops.segment_sum(jnp.ones((idx_dst.shape[0],), feat_src.dtype), idx_dst, num_segments=num_nodes)
            return summed / jnp.maximum(cnt, 1.0)[:, None]
        key = jax.random.key(seed)
        ks = jax.random.split(key, 8)
        s = 1.0 / np.sqrt(D_IN)
        return {'x': jax.random.normal(ks[0], (N, D_IN), jnp.float32), 'edge_index': jax.random.randint(ks[1], (2, E), 0, N, dtype=jnp.int32), 'W_self': jax.random.uniform(ks[2], (D_IN, D_OUT), jnp.float32, -s, s), 'b_self': jax.random.uniform(ks[3], (D_OUT,), jnp.float32, -s, s), 'W_s2d': jax.random.uniform(ks[4], (D_IN, D_OUT), jnp.float32, -s, s), 'b_s2d': jax.random.uniform(ks[5], (D_OUT,), jnp.float32, -s, s), 'W_d2s': jax.random.uniform(ks[6], (D_IN, D_OUT), jnp.float32, -s, s), 'b_d2s': jax.random.uniform(ks[7], (D_OUT,), jnp.float32, -s, s)}
    _L2_gnn_all = _L2_gnn_setup()
    _L2_gnn_in = {k: v for k, v in _L2_gnn_all.items() if k in ('W_self', 'b_self', 'W_s2d', 'b_s2d', 'W_d2s', 'b_d2s')}
    del _L2_gnn_all

    def _L3_gnn_setup():
        import jax, jax.numpy as jnp
        import numpy as np
        N = 6250
        E = 100000
        IN_FEATS = 64
        HIDDEN = 256
        OUT_FEATS = 64
        key = jax.random.key(seed)
        k_x, k_src, k_dst, k_w1, k_b1, k_w2, k_b2 = jax.random.split(key, 7)
        x = jax.random.normal(k_x, (N, IN_FEATS), dtype=jnp.float32)
        src = jax.random.randint(k_src, (E,), 0, N, dtype=jnp.int32)
        dst = jax.random.randint(k_dst, (E,), 0, N, dtype=jnp.int32)
        s1 = 1.0 / np.sqrt(IN_FEATS)
        s2 = 1.0 / np.sqrt(HIDDEN)
        W1 = jax.random.uniform(k_w1, (IN_FEATS, HIDDEN), jnp.float32, -s1, s1)
        b1 = jax.random.uniform(k_b1, (HIDDEN,), jnp.float32, -s1, s1)
        W2 = jax.random.uniform(k_w2, (HIDDEN, OUT_FEATS), jnp.float32, -s2, s2)
        b2 = jax.random.uniform(k_b2, (OUT_FEATS,), jnp.float32, -s2, s2)
        eps = jnp.zeros((1,), dtype=jnp.float32)
        return {'x': x, 'W1': W1, 'b1': b1, 'W2': W2, 'b2': b2, 'eps': eps, 'src': src, 'dst': dst}
    _L3_gnn_all = _L3_gnn_setup()
    _L3_gnn_in = {k: v for k, v in _L3_gnn_all.items() if k in ('W1', 'b1', 'W2', 'b2', 'eps')}
    del _L3_gnn_all
    return {'x': x, 'src': src, 'dst': dst, 'edge_attr_64': edge_attr_64, 'node_vec1': node_vec1, 'node_vec1_n2': node_vec1_n2, 'L0_gnn_ps_w': _L0_gnn_in['ps_w'], 'L1_gnn_W1_l': _L1_gnn_in['W1_l'], 'L1_gnn_b1': _L1_gnn_in['b1'], 'L1_gnn_W1_r': _L1_gnn_in['W1_r'], 'L1_gnn_W2_l': _L1_gnn_in['W2_l'], 'L1_gnn_b2': _L1_gnn_in['b2'], 'L1_gnn_W2_r': _L1_gnn_in['W2_r'], 'L2_gnn_W_self': _L2_gnn_in['W_self'], 'L2_gnn_b_self': _L2_gnn_in['b_self'], 'L2_gnn_W_s2d': _L2_gnn_in['W_s2d'], 'L2_gnn_b_s2d': _L2_gnn_in['b_s2d'], 'L2_gnn_W_d2s': _L2_gnn_in['W_d2s'], 'L2_gnn_b_d2s': _L2_gnn_in['b_d2s'], 'L3_gnn_W1': _L3_gnn_in['W1'], 'L3_gnn_b1': _L3_gnn_in['b1'], 'L3_gnn_W2': _L3_gnn_in['W2'], 'L3_gnn_b2': _L3_gnn_in['b2'], 'L3_gnn_eps': _L3_gnn_in['eps']}

def reference(x, src, dst, edge_attr_64, node_vec1, node_vec1_n2, L0_gnn_ps_w, L1_gnn_W1_l, L1_gnn_b1, L1_gnn_W1_r, L1_gnn_W2_l, L1_gnn_b2, L1_gnn_W2_r, L2_gnn_W_self, L2_gnn_b_self, L2_gnn_W_s2d, L2_gnn_b_s2d, L2_gnn_W_d2s, L2_gnn_b_d2s, L3_gnn_W1, L3_gnn_b1, L3_gnn_W2, L3_gnn_b2, L3_gnn_eps):
    import jax
    import jax.numpy as jnp

    def _L0_gnn_ref(weight, ps_w, review_feat, cj, ci, src, dst):
        import jax, jax.numpy as jnp
        import numpy as np
        N = 12500
        E = 400000
        D = 64
        feat = weight * cj
        pa = jax.nn.sigmoid(review_feat @ ps_w.T)
        msg = pa * feat[src]
        h = jax.ops.segment_sum(msg, dst, num_segments=weight.shape[0])
        return h * ci

    def _L1_gnn_ref(x, edge_index, W1_l, b1, W1_r, W2_l, b2, W2_r):
        import jax, jax.numpy as jnp
        import numpy as np
        N_NODES = 12500
        N_EDGES = 156250
        D_IN, D_HID, D_OUT = (64, 64, 64)

        def _sage_conv(x, edge_index, W_l, b_l, W_r, num_nodes):
            src, dst = (edge_index[0], edge_index[1])
            msgs = x[src]
            agg = jax.ops.segment_sum(msgs, dst, num_segments=num_nodes)
            cnt = jax.ops.segment_sum(jnp.ones((src.shape[0],), x.dtype), dst, num_segments=num_nodes)
            mean = agg / jnp.maximum(cnt, 1.0)[:, None]
            return mean @ W_l.T + b_l + x @ W_r.T
        n = x.shape[0]
        h = _sage_conv(x, edge_index, W1_l, b1, W1_r, n)
        h = jax.nn.relu(h)
        out = _sage_conv(h, edge_index, W2_l, b2, W2_r, n)
        return out

    def _L2_gnn_ref(x, edge_index, W_self, b_self, W_s2d, b_s2d, W_d2s, b_d2s):
        import jax, jax.numpy as jnp
        import numpy as np
        N = 12500
        E = 200000
        D_IN = 64
        D_OUT = 64
        ALPHA = 0.5

        def _mean_agg(feat_src, idx_dst, num_nodes):
            summed = jax.ops.segment_sum(feat_src, idx_dst, num_segments=num_nodes)
            cnt = jax.ops.segment_sum(jnp.ones((idx_dst.shape[0],), feat_src.dtype), idx_dst, num_segments=num_nodes)
            return summed / jnp.maximum(cnt, 1.0)[:, None]
        src, dst = (edge_index[0], edge_index[1])
        n = x.shape[0]
        agg_in = _mean_agg(x[src], dst, n)
        agg_out = _mean_agg(x[dst], src, n)
        out = x @ W_self + b_self + (1.0 - ALPHA) * (agg_in @ W_s2d + b_s2d) + ALPHA * (agg_out @ W_d2s + b_d2s)
        return out

    def _L3_gnn_ref(x, W1, b1, W2, b2, eps, src, dst):
        import jax, jax.numpy as jnp
        import numpy as np
        N = 6250
        E = 100000
        IN_FEATS = 64
        HIDDEN = 256
        OUT_FEATS = 64
        agg = jax.ops.segment_sum(x[src], dst, num_segments=x.shape[0])
        h = agg + (1.0 + eps) * x
        h = h @ W1 + b1
        return h @ W2 + b2
    edge_index = jnp.stack([src, dst])
    x = _layernorm(x + _L0_gnn_ref(x, L0_gnn_ps_w, edge_attr_64, node_vec1, node_vec1_n2, src, dst), axis=-1)
    x = _layernorm(x + _L1_gnn_ref(x, edge_index, L1_gnn_W1_l, L1_gnn_b1, L1_gnn_W1_r, L1_gnn_W2_l, L1_gnn_b2, L1_gnn_W2_r), axis=-1)
    x = _layernorm(x + _L2_gnn_ref(x, edge_index, L2_gnn_W_self, L2_gnn_b_self, L2_gnn_W_s2d, L2_gnn_b_s2d, L2_gnn_W_d2s, L2_gnn_b_d2s), axis=-1)
    x = _layernorm(x + _L3_gnn_ref(x, L3_gnn_W1, L3_gnn_b1, L3_gnn_W2, L3_gnn_b2, L3_gnn_eps, src, dst), axis=-1)
    return x

_drawn_inputs = setup_inputs


def setup_inputs(seed=0):
    import zlib

    import numpy as np

    out = dict(_drawn_inputs(seed))
    spreads = {'L1_gnn_b1': (0.0, 0.1), 'L1_gnn_b2': (0.0, 0.1)}
    factors = {'L3_gnn_b1': 8.0, 'L3_gnn_b2': 8.0}
    for name, (base, spread) in spreads.items():
        noise = np.random.default_rng([zlib.crc32(name.encode()), seed]).standard_normal(out[name].shape)
        drawn = base * np.exp(spread * noise) if base else spread * noise
        out[name] = jnp.asarray(drawn.astype(out[name].dtype))
    for name, factor in factors.items():
        out[name] = (out[name] * factor).astype(out[name].dtype)
    return out
```

```python
from contextlib import ExitStack

import concourse.bass as bass
from concourse import mybir

F32 = mybir.dt.float32
BF16 = mybir.dt.bfloat16
I32 = mybir.dt.int32
ALU = mybir.AluOpType
ACT = mybir.ActivationFunctionType
AX = mybir.AxisListType.X

P = 128
N, E, D = 6250, 206250, 64
BN = 125
NB = N // BN
WN = 5
WB = BN // WN
WGRP = -(-NB * WB // P)
WT = 2
WE = WT * P
KW = NB * WN
BT = 36
BE = BT * P
ROWS = 1650
EP = ROWS * P
SAMP = -(-E // P)
EPP = E // P
TAIL = E - EPP * P
TCOLS = WGRP + 1
FAR = 20000.0
MAGIC = 12582912.0
LN_EPS = 1e-5
XW = 3 * D + 1
XP = XW + 1
RING = 5
EA = 108
OG = 5
LG = 12


class Count:

    def __init__(self, sem):
        self.sem, self.base, self.n = sem, 0, 0

    def __call__(self, ins):
        ins.then_inc(self.sem, 1)
        self.n += 1
        return self.base + self.n

    @property
    def now(self):
        return self.base + self.n

    def enter(self, i, per):
        self.start = self.now
        self.per = per
        self.base, self.n = self.start + i * per if per else self.start, 0

    def leave(self, trips):
        assert self.n == self.per, (self.n, self.per)
        self.base, self.n = self.start + trips * self.per, 0


def build(nc, x_t, cj_t, ci_t, src, dst, samples, edge_attr, ps_w, w1, b1, w2, b2, w3, w3o, b3s, b3i, b3o,
          w4a, b4a, w4b, b4b, eps, out):
    src_rows = src.rearrange("(r e) -> r e", e=P)
    dst_rows = dst.rearrange("(r e) -> r e", e=P)
    src_flat = src.rearrange("(a e) -> a e", a=1)
    dst_flat = dst.rearrange("(a e) -> a e", a=1)
    pa_dram = nc.dram_tensor("pa_dram", (EP,), F32).ap()
    pa_flat = pa_dram.rearrange("(a e) -> a e", a=1)
    y_dram = nc.dram_tensor("y_dram", (N, D), F32).ap()
    at_dram = nc.dram_tensor("at_dram", (NB, P, NB * BN), BF16).ap()
    a_dram = nc.dram_tensor("a_dram", (NB, P, NB * BN), BF16).ap()

    with ExitStack() as ctx:
        def sb(name, shape, dt, c=ctx):
            return c.enter_context(nc.sbuf_tensor(name, shape, dt))

        def sem(name):
            return ctx.enter_context(nc.semaphore(name))

        iota_key = sb("iota_key", [P, KW], BF16)
        iota_f = sb("iota_f", [P, BN + 3], F32)
        ident_f = sb("ident_f", [P, P], F32)
        ident_b = sb("ident_b", [P, P], BF16)
        thr_i = sb("thr_i", [P, TCOLS], I32)
        thr = sb("thr", [P, TCOLS], F32)
        cj = sb("cj", [BN, NB], F32)
        ci = sb("ci", [BN, NB], F32)
        psw = sb("psw", [P, D], F32)
        W1 = sb("W1", [P, D], F32)
        W2 = sb("W2", [P, D], F32)
        W3 = sb("W3", [P, D], F32)
        W3o = sb("W3o", [D, D], F32)
        W4a = sb("W4a", [D, 4 * D], F32)
        W4b = sb("W4b", [P, 2, D], F32)
        bias = sb("bias", [P, 6, D], F32)
        b4 = sb("b4", [P, 2], F32)
        ope = sb("ope", [P, 1], F32)
        epsc = sb("epsc", [P, 1], F32)
        cnt = sb("cnt", [P, TCOLS], F32)
        rowf = sb("rowf", [P, TCOLS], F32)
        rowi = sb("rowi", [P, TCOLS], I32)
        below = sb("below", [P, TCOLS], F32)
        starts = sb("starts", [P, TCOLS], I32)
        XS = sb("XS", [BN, NB, D], F32)
        with ExitStack() as early:
            EW = sb("EW", [P, 3, WGRP * WE], F32, early)
        X3 = sb("X3", [P, 2, NB, XP], BF16)
        RC = sb("RC", [BN, NB], F32)
        KEYT = sb("KEYT", [P, WT, WGRP * P], F32)
        LOT = sb("LOT", [P, WT, WGRP * P], F32)
        SRCT = sb("SRCT", [P, BT, NB], F32)
        DLT = sb("DLT", [P, BT, NB], F32)
        PAT = sb("PAT", [P, BT, NB], F32)
        keyc = sb("keyc", [P, 2, WT, WB], F32)
        loc = sb("loc", [P, 2, WT, WB], F32)
        srcc = sb("srcc", [P, 2, BT], I32)
        dlc = sb("dlc", [P, 2, BT], F32)
        pac = sb("pac", [P, 2, BT], F32)
        lnst = sb("lnst", [BN, 6], F32)
        lnmv = sb("lnmv", [BN, 2], F32)
        lnsd = sb("lnsd", [BN, 1], F32)
        lnrs = sb("lnrs", [BN, 1], F32)
        Z = sb("Z", [BN, D], F32)
        R = sb("R", [BN, D], F32)
        with ExitStack() as pro:
            ea = sb("ea", [P, 2, EA, D], F32, pro)
            T1 = sb("T1", [P, WGRP, WE], F32, pro)
            T3 = sb("T3", [P, WGRP, WE], F32, pro)
            BD = sb("BD", [NB, BE], F32, pro)
            zpad = sb("zpad", [50, (EP - E) // 50], F32, pro)
            iota_i = sb("iota_i", [P, KW], I32, pro)
            tail = sb("tail", [TAIL, D], F32, pro)
            tdot = sb("tdot", [TAIL, 1], F32, pro)
            dot = sb("dot", [P, EPP], F32, pro)
        slots = sb("slots", [P, RING, NB * BN], BF16)
        with ExitStack() as lay0:
            G = sb("G", [P, 2, BT, D], F32, lay0)
            KOH = sb("KOH", [P, 4 * OG, KW], BF16, lay0)
            LOH = sb("LOH", [P, 4 * OG, P], BF16, lay0)
            OHW = sb("OHW", [P, 2 * LG, BN], F32, lay0)
        HS = sb("HS", [BN, NB, D], F32)
        OUTS = sb("OUTS", [BN, NB, D], F32)
        MX = sb("MX", [BN, RING, 2 * D], F32)
        MO = sb("MO", [BN, RING, D], F32)
        AG = sb("AG", [BN, D + 2], F32)
        TS = sb("TS", [P, 2, P], F32)
        H1 = sb("H1", [P, 2, BN], F32)
        PS = ctx.enter_context(nc.psum_tensor("PS", [P, 8, 512], F32))

        win_of = [EW[:, k, :].rearrange("p (g e) -> p g e", e=WE) for k in range(3)]
        WDF, WSF, T2 = win_of
        WD, WS = WDF.bitcast(I32), WSF.bitcast(I32)
        samp_i = T1[:, :, :].rearrange("p g e -> p (g e)")[:, 0:SAMP].bitcast(I32)
        samp_f = T3[:, :, :].rearrange("p g e -> p (g e)")[:, 0:SAMP]
        mask = EW[:, 2, 0:SAMP]
        low = EW[:, 0, 0:TCOLS * P].rearrange("p (g e) -> p g e", e=P)
        low_i = low.bitcast(I32)
        BS = ea[0:NB, 0, :, :].rearrange("p a b -> p (a b)")[:, 0:BE]
        BP = ea[0:NB, 1, :, :].rearrange("p a b -> p (a b)")[:, 0:BE]
        HB = NB // 2
        y_half = [t[0:BN, :, :].rearrange("p a b -> p (a b)")[:, 0:HB * D].rearrange("p (b d) -> p b d", d=D)
                  for t in (SRCT, DLT)]

        in_x, in_w, in_samp, in_tail = sem("in_x"), sem("in_w"), sem("in_samp"), sem("in_tail")
        in_ea = [sem("in_ea0"), sem("in_ea1")]
        iota_done = sem("iota_done")
        dve_step = sem("dve_step")
        settled_waits = sem("settled_waits")
        sig_done = sem("sig_done")
        y_stored, pa_stored = sem("y_stored"), sem("pa_stored")
        low_in, win_in, blk_in, pa_in = sem("low_in"), sem("win_in"), sem("blk_in"), sem("pa_in")
        col_ready = sem("col_ready")
        col_out = sem("col_out")

        cols = sem("cols")
        oh_ready = sem("oh_ready")
        win_ready = sem("win_ready")
        win_out = sem("win_out")
        tr_ready = sem("tr_ready")
        tr_out = sem("tr_out")
        ow_ready = sem("ow_ready")
        ow_used = sem("ow_used")
        h0_taken = sem("h0_taken")
        at_stored = [sem("at_stored0"), sem("at_stored1")]
        a_stored = [sem("a_stored0"), sem("a_stored1")]
        rows_in = [sem("rows_in0"), sem("rows_in1")]
        mv_ready = sem("mv_ready")
        sd_ready = sem("sd_ready")
        x3_ready = sem("x3_ready")

        slot_in = [sem(f"slot_in{u}") for u in range(RING)]
        slot_used = [sem(f"slot_used{u}") for u in range(RING)]
        agg_taken = sem("agg_taken")
        row_ready = sem("row_ready")
        mt_ready = sem("mt_ready")
        ts_ready = sem("ts_ready")
        h1_ready = sem("h1_ready")
        h1_out = sem("h1_out")
        o_ready = sem("o_ready")
        o_taken = sem("o_taken")
        out_ready = sem("out_ready")
        out_stored = sem("out_stored")

        CH = [(o, min(EA, EPP - o)) for o in range(0, EPP, EA)]
        V = {}
        batches = [("win", a, h, list(range(g, min(g + 4, WGRP)))) for a in range(2) for h in range(WT)
                   for g in range(0, WGRP, 4)]
        batches += [("blk", a, 0, list(range(t, t + 9))) for a in range(3) for t in range(0, BT, 9)]
        NBAT = len(batches)
        GR, LR = WB // OG, BT // LG
        BANKS = ((0, 1), (2, 3), (4,))
        NBK = len(BANKS)
        WOUT = GR * NBK
        TB = 8
        TROUT = -(-NB // TB)
        COLS = 5
        NG = NB // RING
        F_OF = {0: 0, 1: 1, 3: 2, 4: 3}
        TS0 = {0: 0, 1: NB, 3: 2 * NB, 4: 4 * NB}
        NORM0 = {1: NB, 3: 2 * NB, 4: 3 * NB}
        X_IN = (0, 1, 0, 0, 1)
        X_NEED = (NB, 2 * NB, 3 * NB, 3 * NB, 4 * NB)

        def settled(e):
            e.sem_inc(settled_waits, 1)

        block = ctx.enter_context(nc.Block())

        @block.vector
        def _(e):
            st = Count(dve_step)

            def step(ins, wait=True):
                v = st(ins)
                if wait:
                    e.wait_ge(dve_step, v)
                return v

            def mark(c, ins):
                v = c(ins)
                e.wait_ge(c.sem, v)

            e.wait_ge(iota_done, 2)
            step(e.tensor_copy(iota_key[:, :], iota_i[:, :]), False)
            step(e.tensor_copy(iota_f[:, :], iota_i[:, 0:BN + 3]), False)
            step(e.tensor_copy(ident_b[:, :], ident_f[:, :]), False)
            step(e.memset(epsc[:, :], LN_EPS), False)
            step(e.tensor_copy(thr[:, :], thr_i[:, :]))
            e.wait_ge(in_samp, 16)
            step(e.tensor_copy(samp_f, samp_i))
            for g in range(TCOLS):
                step(e.tensor_scalar(mask, samp_f, thr[:, g:g + 1], None, ALU.is_lt))
                step(e.tensor_reduce(cnt[:, g:g + 1], mask, AX, ALU.add))
            step(e.tensor_scalar(rowf[:, :], cnt[:, :], 1.0, 0.0, ALU.subtract, ALU.max))
            step(e.tensor_copy(rowi[:, :], rowf[:, :]))
            V["rows"] = st.now
            e.wait_ge(in_x, 48)
            for half in range(2):
                s = slice(half * HB, half * HB + HB)
                step(e.tensor_tensor(y_half[half], XS[:, s, :], cj[:, s].unsqueeze(2).to_broadcast([BN, HB, D]), ALU.mult), False)
            V["y"] = st.now
            e.wait_ge(in_w, 16 * 15)
            step(e.tensor_scalar(W3[0:D, :], W3[0:D, :], 0.5, None, ALU.mult), False)
            step(e.tensor_scalar(W3o[:, :], W3o[:, :], 0.5, None, ALU.mult), False)
            step(e.tensor_scalar(ope[:, :], ope[:, :], 1.0, None, ALU.add), False)
            step(e.tensor_tensor(bias[:, 3, :], bias[:, 3, :], bias[:, 4, :], ALU.add))
            step(e.scalar_tensor_tensor(bias[:, 2, :], bias[:, 3, :], 0.5, bias[:, 2, :], ALU.mult, ALU.add))
            e.wait_ge(low_in, 16 * TCOLS)
            step(e.tensor_copy(low, low_i))
            step(e.tensor_tensor(low, low, thr[:, :].unsqueeze(2).to_broadcast([P, TCOLS, P]), ALU.is_lt))
            step(e.tensor_reduce(below[:, :], low, AX, ALU.add))
            step(e.scalar_tensor_tensor(below[:, :], rowf[:, :], float(P), below[:, :], ALU.mult, ALU.add))
            step(e.tensor_copy(starts[:, :], below[:, :]))
            V["starts"] = st.now
            V["dot"] = []

            def dots(c):
                o, n = CH[c]
                e.wait_ge(in_ea[c % 2], 16 * (c // 2 + 1))
                chunk = ea[:, c % 2, 0:n, :]
                step(e.tensor_tensor(chunk, chunk, psw[:, :].unsqueeze(1).to_broadcast([P, n, D]), ALU.mult))
                V["dot"].append(step(e.tensor_reduce(dot[:, o:o + n], chunk, AX, ALU.add), False))

            dots(0)
            dots(1)
            e.wait_ge(in_tail, 16)
            step(e.tensor_tensor(tail[:, :], tail[:, :], psw[0:TAIL, :], ALU.mult))
            V["tdot"] = step(e.tensor_reduce(tdot[:, :], tail[:, :], AX, ALU.add), False)
            e.wait_ge(win_in, 16 * 2 * WGRP)
            step(e.tensor_copy(T1[:, :, :], WS))
            step(e.tensor_scalar(T2, T1[:, :, :], 1.0 / BN, 0.5 / BN - 0.5, ALU.mult, ALU.add))
            step(e.tensor_scalar(T2, T2, MAGIC, None, ALU.add))
            step(e.tensor_scalar(T2, T2, MAGIC, None, ALU.subtract))
            step(e.scalar_tensor_tensor(T1[:, :, :], T2, -float(BN), T1[:, :, :], ALU.mult, ALU.add), False)
            step(e.tensor_copy(T3[:, :, :], WD))
            step(e.tensor_tensor(T3[:, :, :], T3[:, :, :], thr[:, 0:WGRP].unsqueeze(2).to_broadcast([P, WGRP, WE]), ALU.subtract))
            step(e.tensor_scalar(WDF, T3[:, :, :], 0.0, FAR, ALU.is_lt, ALU.mult), False)
            step(e.tensor_scalar(WSF, T3[:, :, :], WN - 0.5, FAR, ALU.is_gt, ALU.mult))
            step(e.scalar_tensor_tensor(T3[:, :, :], T2, float(WN), T3[:, :, :], ALU.mult, ALU.add))
            step(e.tensor_tensor(T3[:, :, :], T3[:, :, :], WDF, ALU.add))
            step(e.tensor_tensor(T3[:, :, :], T3[:, :, :], WSF, ALU.add))
            V["keys"] = st.now
            step(e.memset(X3[:, :, :, 0:XW - 1], 0.0), False)
            step(e.memset(X3[:, :, :, XW - 1:XP], 1.0), False)
            for c in range(2, len(CH)):
                dots(c)
            V["ea_read"] = st.now
            e.wait_ge(blk_in, 32)
            step(e.tensor_copy(BD[:, :], BD[:, :].bitcast(I32)))
            step(e.tensor_scalar(BD[:, :], BD[:, :], thr[0:NB, WGRP:TCOLS], None, ALU.subtract), False)
            step(e.tensor_copy(BS, BS.bitcast(I32)))
            V["blocks"] = st.now
            e.wait_ge(col_ready, NBAT)
            step(e.memset(slots[:, 0:4, :], 0.0))
            V["slots"] = st.now

            ohr, owr, taken = Count(oh_ready), Count(ow_ready), Count(h0_taken)
            mvr, x3r = Count(mv_ready), Count(x3_ready)
            aggt, ot, rowr, outr = Count(agg_taken), Count(o_taken), Count(row_ready), Count(out_ready)
            e.sem_inc(oh_ready, GR)
            e.sem_inc(ow_ready, LR)
            e.sem_inc(h0_taken, 2)
            taken.base = 2

            def at(t, j):
                return t[:, bass.ds(j, 1), :].rearrange("p a d -> p (a d)")

            def layer_norm(to, last=None):
                step(e.bn_stats(lnst[:, :], Z[:, :]))
                settled(e)
                v = mvr(e.bn_aggr(lnmv[:, :], lnst[:, :]))
                e.wait_ge(sd_ready, v)
                step(e.reciprocal(lnrs[:, :], lnsd[:, :]))
                ins = e.tensor_scalar(to, Z[:, :], lnmv[:, 0:1], lnrs[:, 0:1], ALU.subtract, ALU.mult)
                mark(last, ins) if last else step(ins)

            def split(v, j, k):
                row = X3[0:BN, k, bass.ds(j, 1), :].rearrange("p a d -> p (a d)")
                part = [row[:, q * D:(q + 1) * D] for q in range(3)]
                step(e.tensor_copy(part[0], v))
                step(e.tensor_tensor(R[:, :], v, part[0], ALU.subtract))
                step(e.tensor_copy(part[1], R[:, :]))
                x3r(e.tensor_tensor(part[2], R[:, :], part[1], ALU.subtract))

            counts = (st, mvr, x3r, aggt, ot, rowr, outr, taken, ohr, owr)

            def loop(trips, body):
                grow = body.grow
                with e.Fori(0, trips) as i:
                    for c, n in zip(counts, grow):
                        c.enter(i, n)
                    body(i)
                    for c in counts:
                        c.leave(trips)

            def build_turn(i):
                for b in range(2):
                    j = 2 * i + b
                    e.wait_ge(cols, COLS * (j + 1))
                    for g in range(GR):
                        n = b * GR + g
                        half = n % 2
                        e.wait_ge(win_ready, NBK * (2 * GR * i + n))
                        for w in range(OG):
                            for h in range(WT):
                                t = (half * OG + w) * WT + h
                                W = g * OG + w
                                e.tensor_scalar(KOH[:, t, :], iota_key[:, :], keyc[:, b, h, W:W + 1], None, ALU.is_equal)
                                ins = e.tensor_scalar(LOH[:, t, :], iota_key[:, 0:P], loc[:, b, h, W:W + 1], None, ALU.is_equal)
                        ohr(ins)
                    for g in range(LR):
                        n = b * LR + g
                        e.wait_ge(ow_used, 2 * LR * i + n + LR - 1)
                        for q in range(LG):
                            t = g * LG + q
                            ins = e.tensor_scalar(OHW[:, (n % 2) * LG + q, :], iota_f[:, 0:BN], dlc[:, b, t:t + 1],
                                                  pac[:, b, t:t + 1], ALU.is_equal, ALU.mult)
                        owr(ins)
                    e.wait_ge(ow_used, LR * (j + 2))
                    mark(taken, e.scalar_tensor_tensor(Z[:, :], PS[0:BN, 5 + b, 0:D], ci[:, bass.ds(j, 1)], at(XS, j),
                                                       ALU.mult, ALU.add))
                    layer_norm(at(XS, j))
                    split(at(XS, j), j, 0)

            build_turn.grow = (2 * 6, 2, 2, 0, 0, 0, 0, 2, 2 * GR, 2 * LR)
            loop(NB // 2, build_turn)

            def gather_in(p, j, u):
                inv = AG[:, D + 1:D + 2] if p == 3 else RC[:, bass.ds(j, 1)]
                if p in (0, 3):
                    step(e.tensor_scalar(AG[:, D:D + 1], PS[0:BN, u, 3 * D:XW], 1.0, None, ALU.max))
                    step(e.reciprocal(inv, AG[:, D:D + 1]), False)
                mark(aggt, e.tensor_reduce(AG[:, 0:D], PS[0:BN, u, 0:3 * D].rearrange("p (q d) -> p d q", d=D), AX, ALU.add))
                if p < 2:
                    step(e.tensor_copy(MX[:, u, D:2 * D], at(XS if p == 0 else HS, j)), False)
                    mark(rowr, e.tensor_scalar(MX[:, u, 0:D], AG[:, 0:D], inv, None, ALU.mult))
                elif p == 2:
                    step(e.tensor_scalar(at(HS, j), AG[:, 0:D], inv, None, ALU.mult))
                elif p == 3:
                    step(e.tensor_copy(MX[:, u, 0:D], at(HS, j)), False)
                    step(e.tensor_copy(MX[:, u, D:2 * D], at(XS, j)), False)
                    mark(rowr, e.tensor_scalar(MO[:, u, :], AG[:, 0:D], inv, None, ALU.mult))
                else:
                    mark(rowr, e.scalar_tensor_tensor(MX[:, u, 0:D], at(XS, j), ope[0:BN, 0:1], AG[:, 0:D], ALU.mult, ALU.add))

            def finish(p, j):
                n = {0: 0, 1: 1, 3: 2, 4: 5}[p]
                mark(ot, e.tensor_tensor(Z[:, :], PS[0:BN, 7, 0:D], bias[0:BN, n, :], ALU.add))
                if p == 0:
                    step(e.tensor_scalar(at(HS, j), Z[:, :], 0.0, None, ALU.max))
                    split(at(HS, j), j, 1)
                    return
                step(e.tensor_tensor(Z[:, :], Z[:, :], at(XS, j), ALU.add))
                layer_norm(at(XS if p < 4 else OUTS, j), outr if p == 4 else None)
                if p < 4:
                    split(at(XS, j), j, 0 if p == 1 else 1)

            GROW = {0: (3 + 4, 0, 1, 1, 1, 1, 0), 1: (1 + 7, 1, 1, 1, 1, 1, 0), 2: (1, 0, 0, 1, 0, 0, 0),
                    3: (4 + 7, 1, 1, 1, 1, 1, 0), 4: (0 + 3, 1, 0, 1, 1, 1, 1)}
            for p in range(5):
                def turn(g, gather, fin, p=p):
                    for u in range(RING):
                        if gather and p != 3:
                            e.wait_ge(slot_used[u], NG * p + g + 1)
                            gather_in(p, RING * g + u, u)
                        if fin:
                            j = RING * (g - 1) + u
                            e.wait_ge(o_ready, NB * F_OF[p] + j + 1)
                            finish(p, j)
                    if gather and p == 3:
                        e.wait_ge(slot_used[RING - 1], NG * p + g + 1)
                        for u in range(RING):
                            gather_in(p, RING * g + u, u)

                turn(0, True, False)

                def body(i, p=p):
                    turn(i + 1, True, p != 2)

                body.grow = tuple(RING * n for n in GROW[p]) + (0, 0, 0)
                loop(NG - 1, body)
                if p != 2:
                    turn(NG, False, True)

        @block.gpsimd
        def _(e):
            e.iota(iota_i[:, :], pattern=[[1, KW]], base=0, channel_multiplier=0)
            e.iota(thr_i[:, 0:WGRP], pattern=[[WN * P, WGRP]], base=0, channel_multiplier=WN)
            e.iota(thr_i[:, WGRP:TCOLS], pattern=[[0, 1]], base=0, channel_multiplier=BN)
            e.memset(zpad[:, :], 0.0)
            e.memset(ident_f[:, :], 0.0).then_inc(iota_done, 1)
            e.wait_ge(iota_done, 1)
            e.affine_select(out=ident_f[:, :], in_=ident_f[:, :], compare_op=ALU.not_equal, fill=1.0,
                            base=0, pattern=[[-1, P]], channel_multiplier=1).then_inc(iota_done, 1)

            def gather(to, table, index, axis, s):
                e.indirect_dma_start(out=to, out_offset=None, in_=table,
                                     in_offset=bass.IndirectOffsetOnAxis(ap=index, axis=axis)).then_inc(s, 16)

            e.wait_ge(dve_step, V["rows"])
            for g in range(TCOLS):
                gather(low_i[:, g, :], dst_rows, rowi[:, g:g + 1], 0, low_in)
            e.wait_ge(dve_step, V["starts"])
            for g in range(WGRP):
                gather(WD[:, g, :], dst_flat, starts[:, g:g + 1], 1, win_in)
                gather(WS[:, g, :], src_flat, starts[:, g:g + 1], 1, win_in)
            first = starts[0:NB, WGRP:TCOLS]
            gather(BD[:, :].bitcast(I32), dst_flat, first, 1, blk_in)
            e.wait_ge(dve_step, V["ea_read"])
            gather(BS.bitcast(I32), src_flat, first, 1, blk_in)
            e.wait_ge(pa_stored, 48)
            gather(BP, pa_flat, first, 1, pa_in)
            e.wait_ge(y_stored, 32)
            e.wait_ge(col_ready, NBAT)
            with e.Fori(0, NB // 2) as i:
                for b in range(2):
                    e.wait_ge(cols, COLS * (2 * i + b + 1))
                    e.wait_ge(ow_used, LR * (2 * i + b))
                    settled(e)
                    for t in range(BT):
                        gather(G[:, b, t, :], y_dram, srcc[:, b, t:t + 1], 0, rows_in[b])
            outv = out.rearrange("(b p) d -> p b d", p=BN)
            with e.Fori(0, NG) as g:
                e.wait_ge(out_ready, RING * (g + 1))
                e.dma_start(outv[:, bass.ds(RING * g, RING), :], OUTS[:, bass.ds(RING * g, RING), :]).then_inc(out_stored, 16)
            e.wait_ge(out_stored, 16 * NG)

        @block.sync
        def _(e):
            e.dma_start(samp_i, samples.rearrange("(a s) -> a s", a=1).to_broadcast([P, SAMP])).then_inc(in_samp, 16)
            e.dma_start(psw[:, :], ps_w.to_broadcast([P, D])).then_inc(in_w, 16)
            e.dma_start(XS[:, :, :], x_t).then_inc(in_x, 16)
            e.dma_start(cj[:, :], cj_t).then_inc(in_x, 16)
            e.dma_start(ci[:, :], ci_t).then_inc(in_x, 16)
            with nc.allow_non_contiguous_dma(reason="a bias as a column"):
                for to, frm in ((W1[:, :], w1), (W2[:, :], w2), (W3[:, :], w3), (W3o[:, :], w3o), (W4a[:, :], w4a),
                                (W4b[:, :, :], w4b.rearrange("(c k) n -> k c n", c=2)),
                                (b4[:, :], b4a.rearrange("(c k) -> k c", c=2))):
                    e.dma_start(to, frm).then_inc(in_w, 16)
            for n, v in enumerate((b1, b2, b3s, b3i, b3o, b4b)):
                e.dma_start(bias[:, n, :], v.rearrange("(a d) -> a d", a=1).to_broadcast([P, D])).then_inc(in_w, 16)
            e.dma_start(ope[:, :], eps.rearrange("(a d) -> a d", a=1).to_broadcast([P, 1])).then_inc(in_w, 16)
            e.dma_start(tail[:, :], edge_attr[EPP * P:E, :]).then_inc(in_tail, 16)
            ea_v = edge_attr[0:EPP * P, :].rearrange("(p n) d -> p n d", n=EPP)
            yv = y_dram.rearrange("(b p) d -> p b d", p=BN)
            for c, (o, n) in enumerate(CH):
                if c >= 2:
                    e.wait_ge(dve_step, V["dot"][c - 2])
                e.dma_start(ea[:, c % 2, 0:n, :], ea_v[:, o:o + n, :]).then_inc(in_ea[c % 2], 16)
                if c == 1:
                    e.wait_ge(dve_step, V["y"])
                    for half in range(2):
                        e.dma_start(yv[:, half * HB:half * HB + HB, :], y_half[half]).then_inc(y_stored, 16)
            e.wait_ge(sig_done, len(CH) + 1)
            e.dma_start(pa_dram[0:EPP * P].rearrange("(p n) -> p n", n=EPP), dot[:, :]).then_inc(pa_stored, 16)
            e.dma_start(pa_dram[EPP * P:E].rearrange("(p n) -> p n", n=1), tdot[:, :]).then_inc(pa_stored, 16)
            e.wait_ge(iota_done, 2)
            e.dma_start(pa_dram[E:EP].rearrange("(p n) -> p n", p=50), zpad[:, :]).then_inc(pa_stored, 16)
            with e.Fori(0, NB // 2) as i:
                for b in range(2):
                    j = 2 * i + b
                    e.wait_ge(win_out, NBK + WOUT * (j + 1))
                    e.dma_start(at_dram[bass.ds(j, 1), :, :].rearrange("a p n -> (a p) n"), slots[:, b, :]).then_inc(at_stored[b], 16)
                    e.wait_ge(tr_out, 2 + TROUT * (j + 1))
                    e.dma_start(a_dram[bass.ds(j, 1), :, :].rearrange("a p n -> (a p) n"), slots[:, 2 + b, :]).then_inc(a_stored[b], 16)
            for s in (*at_stored, *a_stored):
                e.wait_ge(s, 16 * (NB // 2))
            for p in range(5):
                with e.Fori(0, NG) as g:
                    for u in range(RING):
                        e.wait_ge(slot_used[u], g + NG * p)
                        if p == 3:
                            rows = NB // RING
                            to = slots[:, u, :].rearrange("p (j n) -> p j n", n=RING * BN)
                            frm = a_dram[rows * u:rows * (u + 1), :, bass.ds(g * (RING * BN), RING * BN)].rearrange("j p n -> p j n")
                        else:
                            to = slots[:, u, :]
                            frm = at_dram[bass.ds(RING * g + u, 1), :, :].rearrange("a p n -> (a p) n")
                        e.dma_start(to, frm).then_inc(slot_in[u], 16)

        @block.scalar
        def _(e):
            for c, (o, n) in enumerate(CH):
                e.wait_ge(dve_step, V["dot"][c])
                e.activation(dot[:, o:o + n], dot[:, o:o + n], ACT.Sigmoid).then_inc(sig_done, 1)
            e.wait_ge(dve_step, V["tdot"])
            e.activation(tdot[:, :], tdot[:, :], ACT.Sigmoid).then_inc(sig_done, 1)
            e.wait_ge(y_stored, 32)
            for n, (kind, a, h, items) in enumerate(batches):
                e.wait_ge(col_ready, n + 1)
                if kind == "win":
                    to = (KEYT, LOT)[a][:, h, items[0] * P:(items[-1] + 1) * P]
                    k = len(items) * P
                else:
                    to = (DLT, SRCT, PAT)[a][:, items[0]:items[-1] + 1, :].rearrange("p t j -> p (t j)")
                    k = len(items) * NB
                e.activation(to, PS[:, n % 2, 0:k], ACT.Copy).then_inc(col_out, 1)
            e.wait_ge(col_out, NBAT)
            e.wait_ge(dve_step, V["slots"])
            e.sem_inc(win_out, NBK)
            e.sem_inc(tr_out, 2)
            with e.Fori(0, NB // 2) as i:
                for b in range(2):
                    j = 2 * i + b
                    e.wait_ge(oh_ready, GR * j)
                    e.wait_ge(ow_ready, LR * j)
                    e.wait_ge(rows_in[b], 16 * BT * i)
                    window = bass.ds(j * WB, WB)
                    e.activation(keyc[:, b, :, :], KEYT[:, :, window], ACT.Copy).then_inc(cols, 1)
                    e.activation(loc[:, b, :, :], LOT[:, :, window], ACT.Copy).then_inc(cols, 1)
                    for to, frm in ((srcc, SRCT), (dlc, DLT), (pac, PAT)):
                        e.activation(to[:, b, :], frm[:, :, bass.ds(j, 1)].rearrange("p t a -> p (t a)"), ACT.Copy).then_inc(cols, 1)
                    e.wait_ge(at_stored[b], 16 * i)
                    slot = slots[:, b, :].rearrange("p (h w l) -> p w h l", h=NB, l=WN)
                    for g in range(GR):
                        for k, ws in enumerate(BANKS):
                            e.wait_ge(win_ready, NBK + WOUT * j + NBK * g + k + 1)
                            w = OG * g + ws[0]
                            e.activation(slot[:, w:w + len(ws), :, :],
                                         PS[:, k, 0:len(ws) * KW].rearrange("p (w h l) -> p w h l", h=NB, l=WN),
                                         ACT.Copy).then_inc(win_out, 1)
                    e.wait_ge(a_stored[b], 16 * i)
                    slot = slots[0:BN, 2 + b, :].rearrange("p (h l) -> p h l", h=NB)
                    for n in range(TROUT):
                        h0, h1 = TB * n, min(TB * n + TB, NB)
                        e.wait_ge(tr_ready, TROUT * j + n + 1)
                        bank = PS[0:BN, 3 + (b * TROUT + n) % 2, :].bitcast(BF16).rearrange("p (h l) -> p h l", l=P)
                        e.activation(slot[:, h0:h1, :], bank[:, 0:h1 - h0, 0:BN], ACT.Copy).then_inc(tr_out, 1)
                    e.wait_ge(mv_ready, j + 1)
                    e.activation(lnsd[:, :], lnmv[:, 1:2], ACT.Sqrt, bias=epsc[0:BN, 0:1]).then_inc(sd_ready, 1)
            for p in (0, 1, 3, 4):
                with e.Fori(0, NG) as g:
                    for u in range(RING):
                        j = RING * g + u
                        e.wait_ge(mt_ready, NB * F_OF[p] + j + 1)
                        k = D if p == 4 else P
                        e.activation(TS[0:k, 0, 0:BN], PS[0:k, 5, 0:BN], ACT.Copy).then_inc(ts_ready, 1)
                        if p == 3:
                            e.activation(TS[0:D, 1, 0:BN], PS[0:D, 5, P:P + BN], ACT.Copy).then_inc(ts_ready, 1)
                        if p == 4:
                            e.wait_ge(h1_ready, j + 1)
                            for c in range(2):
                                e.activation(H1[:, c, :], PS[:, 6, c * P:c * P + BN], ACT.Identity, bias=b4[:, c:c + 1]).then_inc(h1_out, 1)
                        if p != 0:
                            e.wait_ge(mv_ready, NORM0[p] + j + 1)
                            e.activation(lnsd[:, :], lnmv[:, 1:2], ACT.Sqrt, bias=epsc[0:BN, 0:1]).then_inc(sd_ready, 1)

        @block.tensor
        def _(e):
            for n, (kind, a, h, items) in enumerate(batches):
                if kind == "win":
                    e.wait_ge(dve_step, V["keys"])
                elif a < 2:
                    e.wait_ge(dve_step, V["blocks"])
                else:
                    e.wait_ge(pa_in, 16)
                if n >= 2:
                    e.wait_ge(col_out, n - 1)
                for k, it in enumerate(items):
                    if kind == "win":
                        frm = (T3, T1)[a][:, it, h * P:(h + 1) * P]
                        ins = e.transpose(PS[:, n % 2, k * P:(k + 1) * P], frm, ident_f[:, :])
                    else:
                        frm = (BD[:, :], BS, BP)[a][:, it * P:(it + 1) * P]
                        ins = e.transpose(PS[:, n % 2, k * NB:(k + 1) * NB], frm, ident_f[0:NB, 0:NB])
                ins.then_inc(col_ready, 1)
            e.sem_inc(win_ready, NBK)
            e.sem_inc(ow_used, LR)
            e.wait_ge(col_out, NBAT)
            with e.Fori(0, NB // 2) as i:
                for b in range(2):
                    j = 2 * i + b
                    for g in range(GR):
                        half = (b * GR + g) % 2
                        e.wait_ge(oh_ready, GR * (j + 1) + g + 1)
                        for k, ws in enumerate(BANKS):
                            e.wait_ge(win_out, WOUT * j + NBK * g + k + 1)
                            for q, w in enumerate(ws):
                                for h in range(WT):
                                    t = (half * OG + w) * WT + h
                                    ins = e.matmul(PS[:, k, q * KW:(q + 1) * KW], LOH[:, t, :], KOH[:, t, :], start=h == 0, stop=h == WT - 1)
                            ins.then_inc(win_ready, 1)
                    e.wait_ge(win_out, NBK + WOUT * (j + 1))
                    for n in range(TROUT):
                        e.wait_ge(tr_out, TROUT * j + n + 1)
                        bank = PS[:, 3 + (b * TROUT + n) % 2, :].bitcast(BF16)
                        for k, h in enumerate(range(TB * n, min(TB * n + TB, NB))):
                            ins = e.transpose(bank[0:BN, k * P:k * P + BN], slots[0:BN, b, h * BN:(h + 1) * BN], ident_b[0:BN, 0:BN])
                        ins.then_inc(tr_ready, 1)
                    e.wait_ge(h0_taken, j + 1)
                    e.wait_ge(rows_in[b], 16 * BT * (i + 1))
                    for g in range(LR):
                        e.wait_ge(ow_ready, LR * (j + 1) + g + 1)
                        for q in range(LG):
                            t = g * LG + q
                            ins = e.matmul(PS[0:BN, 5 + b, 0:D], OHW[:, ((b * LR + g) % 2) * LG + q, :], G[:, b, t, :],
                                           start=t == 0, stop=t == BT - 1)
                        ins.then_inc(ow_used, 1)

            for p in range(5):
                x3 = X3[:, X_IN[p], :, :]
                wide = XW if p in (0, 3) else 3 * D

                def turn(g, gather, fin, p=p, x3=x3, wide=wide):
                    for u in range(RING):
                        if fin:
                            f = F_OF[p]
                            j = RING * (g - 1) + u
                            ts = 2 if p == 3 else 1
                            e.wait_ge(row_ready, NB * f + j + 1)
                            e.wait_ge(ts_ready, TS0[p] + ts * j)
                            if p == 4:
                                settled(e)
                                e.transpose(PS[0:D, 5, 0:BN], MX[:, u, 0:D], ident_f[0:BN, 0:BN]).then_inc(mt_ready, 1)
                            else:
                                ins = e.transpose(PS[:, 5, 0:BN], MX[:, u, :], ident_f[0:BN, 0:BN])
                                if p == 3:
                                    ins = e.transpose(PS[0:D, 5, P:P + BN], MO[:, u, :], ident_f[0:BN, 0:BN])
                                ins.then_inc(mt_ready, 1)
                        if gather:
                            e.wait_ge(slot_in[u], 16 * (NG * p + g + 1))
                            if p == 3:
                                if u == 0:
                                    e.wait_ge(agg_taken, NB * p + RING * g)
                            elif not (p == 0 and isinstance(g, int)):
                                e.wait_ge(agg_taken, NB * p + RING * g + u - RING + 1)

                        def products(a, b):
                            for n in range(a, b):
                                if p == 3:
                                    k, q = n // RING, n % RING
                                    m = e.matmul(PS[0:BN, q, 0:wide], slots[:, u, n * BN:(n + 1) * BN], x3[:, u * (NB // RING) + k, 0:wide],
                                                 start=u == 0 and k == 0, stop=u == RING - 1 and k == NB // RING - 1)
                                else:
                                    m = e.matmul(PS[0:BN, u, 0:wide], slots[:, u, n * BN:(n + 1) * BN], x3[:, n, 0:wide],
                                                 start=n == 0, stop=n == NB - 1)
                            if b == NB:
                                m.then_inc(slot_used[u], 1)

                        if gather:
                            products(0, NB // 2)
                        if fin and p == 4:
                            e.wait_ge(ts_ready, TS0[p] + j + 1)
                            e.wait_ge(h1_out, 2 * j)
                            for c in range(2):
                                ins = e.matmul(PS[:, 6, c * P:c * P + BN], W4a[:, c * P:(c + 1) * P], TS[0:D, 0, 0:BN], start=True, stop=True)
                            ins.then_inc(h1_ready, 1)
                        if gather:
                            products(NB // 2, NB)
                        if fin:
                            e.wait_ge(o_taken, NB * f + j)
                            o = PS[0:BN, 7, 0:D]
                            if p == 4:
                                e.wait_ge(h1_out, 2 * (j + 1))
                                e.matmul(o, H1[:, 0, :], W4b[:, 0, :], start=True, stop=False)
                                ins = e.matmul(o, H1[:, 1, :], W4b[:, 1, :], start=False, stop=True)
                            else:
                                e.wait_ge(ts_ready, TS0[p] + ts * (j + 1))
                                W = (W1, W2, None, W3)[p]
                                ins = e.matmul(o, TS[:, 0, 0:BN], W[:, :], start=True, stop=p != 3)
                                if p == 3:
                                    ins = e.matmul(o, TS[0:D, 1, 0:BN], W3o[:, :], start=False, stop=True)
                            ins.then_inc(o_ready, 1)

                e.wait_ge(x3_ready, X_NEED[p])
                turn(0, True, False)
                with e.Fori(0, NG - 1) as i:
                    turn(i + 1, True, p != 2)
                if p != 2:
                    turn(NG, False, True)


def kernel(**inputs):
    import concourse.bacc as bacc
    import numpy as np
    from concourse.bass_utils import run_bass_kernel_spmd

    v = {k: np.asarray(a) for k, a in inputs.items()}

    def nodes(a):
        return np.ascontiguousarray(a.reshape(NB, BN, -1).transpose(1, 0, 2))

    def padded(a, fill):
        return np.concatenate([a, np.full(EP - E, fill, a.dtype)])

    arrays = {
        "x_t": nodes(v["x"]),
        "cj_t": nodes(v["node_vec1"])[:, :, 0],
        "ci_t": nodes(v["node_vec1_n2"])[:, :, 0],
        "src_p": padded(v["src"], 0),
        "dst_p": padded(v["dst"], 2 * N),
        "samples": v["dst"][::P],
        "edge_attr": v["edge_attr_64"],
        "ps_w": v["L0_gnn_ps_w"],
        "w1": np.concatenate([v["L1_gnn_W1_l"].T, v["L1_gnn_W1_r"].T]),
        "b1": v["L1_gnn_b1"],
        "w2": np.concatenate([v["L1_gnn_W2_l"].T, v["L1_gnn_W2_r"].T]),
        "b2": v["L1_gnn_b2"],
        "w3": np.concatenate([v["L2_gnn_W_s2d"], v["L2_gnn_W_self"]]),
        "w3o": v["L2_gnn_W_d2s"],
        "b3s": v["L2_gnn_b_self"],
        "b3i": v["L2_gnn_b_s2d"],
        "b3o": v["L2_gnn_b_d2s"],
        "w4a": v["L3_gnn_W1"],
        "b4a": v["L3_gnn_b1"],
        "w4b": v["L3_gnn_W2"],
        "b4b": v["L3_gnn_b2"],
        "eps": v["L3_gnn_eps"],
    }
    arrays = {k: np.ascontiguousarray(a) for k, a in arrays.items()}
    nc = bacc.Bacc("TRN2", target_bir_lowering=False, num_devices=1)
    args = [nc.dram_tensor(k, a.shape, mybir.dt.from_np(a.dtype), kind="ExternalInput").ap() for k, a in arrays.items()]
    args.append(nc.dram_tensor("out", (N, D), F32, kind="ExternalOutput").ap())
    build(nc, *args)
    return run_bass_kernel_spmd(nc, [arrays], core_ids=[0]).results[0]["out"]
```

```python
from contextlib import ExitStack

import concourse.bass as bass
from concourse import mybir

F32 = mybir.dt.float32
BF16 = mybir.dt.bfloat16
I32 = mybir.dt.int32
F16 = mybir.dt.float16
FP8 = mybir.dt.float8e4
ALU = mybir.AluOpType
ACT = mybir.ActivationFunctionType
AX = mybir.AxisListType.X

P = 128
N, E, D = 6250, 206250, 64
BN = 125
NB = N // BN
WN = 5
WB = BN // WN
WGRP = -(-NB * WB // P)
WT = 2
WE = WT * P
KW = NB * WN
BT = 34
BE = BT * P
TAIL = E - (E // P) * P
ROWS = 1650
EP = ROWS * P
SAMP = -(-E // P)
TCOLS = WGRP + 1
FAR = 20000.0
MAGIC = 12582912.0
LN_EPS = 1e-5
MOST = 15.0
HW = 3 * D
XW = 2 * D + 1
XP = XW + 1
LOW = 4096.0
PITCH = P
RING = 5
OG = 5
LG = 7
OR = 5


NT = SAMP
DUP = 65536.0


class Count:

    def __init__(self, sem):
        self.sem, self.base, self.n = sem, 0, 0

    def __call__(self, ins):
        ins.then_inc(self.sem, 1)
        self.n += 1
        return self.base + self.n

    @property
    def now(self):
        return self.base + self.n

    def enter(self, i, per):
        self.start = self.now
        self.per = per
        self.base, self.n = self.start + i * per if per else self.start, 0

    def leave(self, trips):
        assert self.n == self.per, (self.n, self.per)
        self.base, self.n = self.start + trips * self.per, 0


def build(nc, x_t, cj_t, ci_t, src, dst, samples, edge_attr, ps_w, w1, b1, w2, b2, w3, w3o, b3s, b3i, b3o,
          w4a, b4a, w4b, b4b, eps, out):
    src_rows = src.rearrange("(r e) -> r e", e=P)
    dst_rows = dst.rearrange("(r e) -> r e", e=P)
    src_flat = src.rearrange("(a e) -> a e", a=1)
    dst_flat = dst.rearrange("(a e) -> a e", a=1)
    bst_dram = nc.dram_tensor("bst_dram", (NB + 2, 1), I32).ap()
    wst_dram = nc.dram_tensor("wst_dram", (WGRP * P + 1, 1), F32).ap()
    row_dram = nc.dram_tensor("row_dram", (N, D), F32).ap()
    sum_dram = nc.dram_tensor("sum_dram", (N, HW), F32).ap()
    y_dram = nc.dram_tensor("y_dram", (N, D), F32).ap()
    at_dram = nc.dram_tensor("at_dram", (NB, P, NB * PITCH // 2), BF16).ap()
    a_dram = nc.dram_tensor("a_dram", (NB, P, NB * PITCH // 2), BF16).ap()

    with ExitStack() as ctx:
        def sb(name, shape, dt, c=ctx):
            return c.enter_context(nc.sbuf_tensor(name, shape, dt))

        def sem(name):
            return ctx.enter_context(nc.semaphore(name))

        iota_key = sb("iota_key", [P, KW], BF16)
        iota_f = sb("iota_f", [P, BN + 3], F32)
        ident_f = sb("ident_f", [P, P], F32)
        ident_b = sb("ident_b", [P, P], BF16)
        thr_i = sb("thr_i", [P, TCOLS], I32)
        thr = sb("thr", [P, TCOLS], F32)
        cj = sb("cj", [BN, NB], F32)
        ci = sb("ci", [BN, NB], F32)
        psw = sb("psw", [P, D], F32)
        W1 = sb("W1", [P, D], F32)
        W2 = sb("W2", [P, D], F32)
        W3 = sb("W3", [P, D], F32)
        W3o = sb("W3o", [D, D], F32)
        W4a = sb("W4a", [D, 4 * D], F32)
        W4b = sb("W4b", [P, 2, D], F32)
        bias = sb("bias", [P, 6, D], F32)
        b4 = sb("b4", [P, 2], F32)
        ope = sb("ope", [P, 1], F32)
        epsc = sb("epsc", [P, 1], F32)
        most = sb("most", [P, 1], F32)
        lowt = sb("lowt", [BN, D], F32)
        cnt = sb("cnt", [P, TCOLS], F32)
        rowf = sb("rowf", [P, TCOLS], F32)
        rowi = sb("rowi", [P, TCOLS], I32)
        below = sb("below", [P, TCOLS], F32)
        starts = sb("starts", [P, TCOLS], I32)
        bstart = sb("bstart", [P, 1], I32)
        base = sb("base", [P, NB], F32)
        nxt = sb("nxt", [P, TCOLS], F32)
        total = sb("total", [P, 2], F32)
        slow = sb("slow", [1, 1], I32)
        overc = sb("overc", [P, 2, 5], F32)
        over = sb("over", [P, NB * 5 + 4], F32)
        XS = sb("XS", [BN, NB, D], F32)
        with ExitStack() as early:
            EW = sb("EW", [P, 3, WGRP * WE], F32, early)
        XN = sb("XN", [P, 2, NB, XP], F16)
        with ExitStack() as lay0:
            OHW = sb("OHW", [P, OR * LG, BN], F32, lay0)
        XH = sb("XH", [P, NB, HW], BF16)
        RC = sb("RC", [BN, NB], F32)
        KEYT = sb("KEYT", [P, WT, WGRP * P], F32)
        LOT = sb("LOT", [P, WT, WGRP * P], F32)
        keyc = sb("keyc", [P, 2, WT, WB], F32)
        loc = sb("loc", [P, 2, WT, WB], F32)
        srcc = sb("srcc", [P, 2, BT], I32)
        dstc = sb("dstc", [P, 2, BT], I32)
        dlc = sb("dlc", [P, 2, BT], F32)
        pac = sb("pac", [P, 2, BT], F32)
        lnst = sb("lnst", [BN, 6], F32)
        lnmv = sb("lnmv", [BN, 2], F32)
        lnsd = sb("lnsd", [BN, 1], F32)
        lnrs = sb("lnrs", [BN, 1], F32)
        Z = sb("Z", [BN, D], F32)
        R = sb("R", [BN, D], F32)
        with ExitStack() as pro:
            T1 = sb("T1", [P, WGRP, WE], F32, pro)
            T3 = sb("T3", [P, WGRP, WE], F32, pro)
            iota_i = sb("iota_i", [P, KW], I32, pro)
            base_i = sb("base_i", [P, NB], I32, pro)
            ytile = sb("ytile", [BN, NB, D], F32, pro)
            dord = sb("dord", [P, E // P + 1], I32, pro)
            dgt = sb("dgt", [P, E // P], F32, pro)
            dend = sb("dend", [1, TAIL], I32, pro)
            dendf = sb("dendf", [1, TAIL], F32, pro)
        pairs = sb("pairs", [P, RING, NB * PITCH // 2], BF16)
        slots = pairs[:, :, :].bitcast(FP8)
        with ExitStack() as lay0:
            KOH = sb("KOH", [P, OR * WT * OG, KW], BF16, lay0)
            LOH = sb("LOH", [P, OR * WT * OG, P], BF16, lay0)
            ea = sb("ea", [P, 2, BT, D], F32, lay0)
            G = sb("G", [P, 2, BT, D], F32, lay0)
        HS = sb("HS", [BN, NB, D], F32)
        RP = sb("RP", [BN, D], F32)
        g_far = sb("g_far", [P, 1], I32)
        g_near = sb("g_near", [P, 1], I32)
        g_row = sb("g_row", [P, P], I32)
        g_edge = sb("g_edge", [P, D], F32)
        g_farf = sb("g_farf", [P, 1], F32)
        g_nearf = sb("g_nearf", [P, 1], F32)
        g_rowf = sb("g_rowf", [P, P], F32)
        g_same = sb("g_same", [P, P], F32)
        g_before = sb("g_before", [P, P], F32)
        g_tmp = sb("g_tmp", [P, P], F32)
        g_c = sb("g_c", [P, 4], F32)
        g_idx = sb("g_idx", [P, 3], I32)
        g_got = sb("g_got", [P, D], F32)
        g_msg = sb("g_msg", [P, HW], F32)
        g_acc = sb("g_acc", [P, HW], F32)
        GA = sb("GA", [BN, RING, HW], F32)
        OUTS = sb("OUTS", [BN, NB, D], F32)
        MX = sb("MX", [BN, RING, 2 * D], F32)
        MO = sb("MO", [BN, RING, D], F32)
        AG = sb("AG", [BN, D + 2], F32)
        TS = sb("TS", [P, 2, P], F32)
        H1 = sb("H1", [P, 2, BN], F32)
        PS = ctx.enter_context(nc.psum_tensor("PS", [P, 8, 512], F32))

        win_of = [EW[:, k, :].rearrange("p (g e) -> p g e", e=WE) for k in range(3)]
        WDF, WSF, T2 = win_of
        WD, WS = WDF.bitcast(I32), WSF.bitcast(I32)
        samp_i = T1[:, :, :].rearrange("p g e -> p (g e)")[:, 0:SAMP].bitcast(I32)
        samp_f = T3[:, :, :].rearrange("p g e -> p (g e)")[:, 0:SAMP]
        mask = EW[:, 2, 0:SAMP]
        low = EW[:, 0, 0:TCOLS * P].rearrange("p (g e) -> p g e", e=P)
        low_i = low.bitcast(I32)
        junk = slots[:, RING - 1, :]
        in_x, in_w, in_samp = sem("in_x"), sem("in_w"), sem("in_samp")
        iota_done = sem("iota_done")
        dve_step = sem("dve_step")
        settled_waits = sem("settled_waits")
        y_stored, bst_stored = sem("y_stored"), sem("bst_stored")
        order_in, wst_stored, next_in = sem("order_in"), sem("wst_stored"), sem("next_in")
        total_ready = sem("total_ready")
        total_sum = sem("total_sum")
        slow_ready = sem("slow_ready")
        gz = {n: sem("gen_" + n) for n in ("start", "prep", "edge", "step", "index", "dot", "sig", "msg", "sum",
                                           "added", "next", "block_in", "mv", "sd", "x1", "mask")}
        gz_in, gz_rows, gz_kept = ([sem(f"gen_{n}{c}") for c in range(6)] for n in ("in", "rows", "kept"))
        low_in, win_in = sem("low_in"), sem("win_in")
        src_in = [sem("src_in0"), sem("src_in1")]
        ed_in = [sem("ed_in0"), sem("ed_in1")]
        dot_ready = sem("dot_ready")
        sig_ready = sem("sig_ready")
        checked = sem("checked")
        over_kept = sem("over_kept")
        split_ready = sem("split_ready")
        pool_step = sem("pool_step")
        col_ready = sem("col_ready")
        col_out = sem("col_out")

        cols = sem("cols")
        oh_ready = sem("oh_ready")
        win_ready = sem("win_ready")
        win_out = sem("win_out")
        tr_ready = sem("tr_ready")
        tr_out = sem("tr_out")
        ow_ready = sem("ow_ready")
        ow_used = sem("ow_used")
        h0_taken = sem("h0_taken")
        at_stored = [sem("at_stored0"), sem("at_stored1")]
        a_stored = [sem("a_stored0"), sem("a_stored1")]
        rows_in = [sem("rows_in0"), sem("rows_in1")]
        mv_ready = sem("mv_ready")
        sd_ready = sem("sd_ready")
        x3_ready = sem("x3_ready")

        slot_in = [sem(f"slot_in{u}") for u in range(RING)]
        slot_used = [sem(f"slot_used{u}") for u in range(RING)]
        agg_taken = sem("agg_taken")
        row_ready = sem("row_ready")
        mt_ready = sem("mt_ready")
        ts_ready = sem("ts_ready")
        h1_ready = sem("h1_ready")
        h1_out = sem("h1_out")
        o_ready = sem("o_ready")
        o_taken = sem("o_taken")
        out_ready = sem("out_ready")
        out_stored = sem("out_stored")

        V = {}
        batches = [(a, h, list(range(g, min(g + 4, WGRP)))) for a in range(2) for h in range(WT)
                   for g in range(0, WGRP, 4)]
        NBAT = len(batches)
        GR, LR = WB // OG, -(-BT // LG)
        BANKS = ((0, 1), (2, 3), (4,))
        NBK = len(BANKS)
        WOUT = GR * NBK
        TB = 4
        TROUT = -(-NB // TB)
        CHK = LR
        TSPLIT = [TROUT * g // LR for g in range(LR + 1)]
        COLS = 2
        NG = NB // RING
        PREPS = [NG + 1] + [NG + 1] * 5
        F_OF = {0: 0, 1: 1, 3: 2, 4: 3}
        TS0 = {0: 0, 1: NB, 3: 2 * NB, 4: 4 * NB}
        NORM0 = {1: NB, 3: 2 * NB, 4: 3 * NB}
        X_IN = (XN[:, 0], XH, XN[:, 0], XN[:, 0], XN[:, 1])
        X_NEED = (NB, 2 * NB, 3 * NB, 3 * NB, 4 * NB)

        def settled(e):
            e.sem_inc(settled_waits, 1)

        def need(e, s, v):
            if not isinstance(v, int) or v > 0:
                e.wait_ge(s, v)

        block = ctx.enter_context(nc.Block())

        @block.vector
        def _(e):
            st = Count(dve_step)

            def step(ins, wait=True):
                v = st(ins)
                if wait:
                    e.wait_ge(dve_step, v)
                return v

            def mark(c, ins):
                v = c(ins)
                e.wait_ge(c.sem, v)

            e.wait_ge(iota_done, 2)
            step(e.tensor_copy(iota_key[:, :], iota_i[:, :]), False)
            step(e.tensor_copy(iota_f[:, :], iota_i[:, 0:BN + 3]), False)
            step(e.tensor_copy(ident_b[:, :], ident_f[:, :]), False)
            step(e.tensor_copy(base[:, :], base_i[:, :]), False)
            step(e.memset(epsc[:, :], LN_EPS), False)
            step(e.memset(most[:, :], -MOST), False)
            step(e.tensor_copy(thr[:, :], thr_i[:, :]))
            e.wait_ge(in_samp, 16)
            step(e.tensor_copy(samp_f, samp_i))
            for g in range(TCOLS):
                step(e.tensor_scalar(mask, samp_f, thr[:, g:g + 1], None, ALU.is_lt))
                step(e.tensor_reduce(cnt[:, g:g + 1], mask, AX, ALU.add))
            step(e.tensor_scalar(rowf[:, :], cnt[:, :], 1.0, 0.0, ALU.subtract, ALU.max))
            step(e.tensor_copy(rowi[:, :], rowf[:, :]))
            V["rows"] = st.now
            e.wait_ge(in_x, 48)
            step(e.tensor_tensor(ytile[:, :, :], XS[:, :, :], cj[:, :].unsqueeze(2).to_broadcast([BN, NB, D]), ALU.mult), False)
            V["y"] = st.now
            e.wait_ge(in_w, 16 * 15)
            step(e.tensor_scalar(W3[0:D, :], W3[0:D, :], 0.5, None, ALU.mult), False)
            step(e.tensor_scalar(W3o[:, :], W3o[:, :], 0.5, None, ALU.mult), False)
            step(e.tensor_scalar(ope[:, :], ope[:, :], 1.0, None, ALU.add), False)
            step(e.tensor_tensor(bias[:, 3, :], bias[:, 3, :], bias[:, 4, :], ALU.add))
            step(e.scalar_tensor_tensor(bias[:, 2, :], bias[:, 3, :], 0.5, bias[:, 2, :], ALU.mult, ALU.add))
            e.wait_ge(low_in, 16 * TCOLS)
            step(e.tensor_copy(low, low_i))
            step(e.tensor_tensor(low, low, thr[:, :].unsqueeze(2).to_broadcast([P, TCOLS, P]), ALU.is_lt))
            step(e.tensor_reduce(below[:, :], low, AX, ALU.add))
            step(e.scalar_tensor_tensor(below[:, :], rowf[:, :], float(P), below[:, :], ALU.mult, ALU.add))
            step(e.tensor_copy(starts[:, :], below[:, :]), False)
            step(e.tensor_scalar(bstart[:, :], below[:, WGRP:TCOLS], float(E - BE), None, ALU.min))
            V["starts"] = st.now
            e.wait_ge(win_in, 16 * 2 * WGRP)
            step(e.tensor_copy(T1[:, :, :], WS))
            step(e.tensor_scalar(T2, T1[:, :, :], 1.0 / BN, 0.5 / BN - 0.5, ALU.mult, ALU.add))
            step(e.tensor_scalar(T2, T2, MAGIC, None, ALU.add))
            step(e.tensor_scalar(T2, T2, MAGIC, None, ALU.subtract))
            step(e.scalar_tensor_tensor(T1[:, :, :], T2, -float(BN), T1[:, :, :], ALU.mult, ALU.add), False)
            step(e.tensor_copy(T3[:, :, :], WD))
            step(e.tensor_tensor(T3[:, :, :], T3[:, :, :], thr[:, 0:WGRP].unsqueeze(2).to_broadcast([P, WGRP, WE]), ALU.subtract))
            step(e.tensor_scalar(WDF, T3[:, :, :], 0.0, FAR, ALU.is_lt, ALU.mult), False)
            step(e.tensor_scalar(WSF, T3[:, :, :], WN - 0.5, FAR, ALU.is_gt, ALU.mult))
            step(e.scalar_tensor_tensor(T3[:, :, :], T2, float(WN), T3[:, :, :], ALU.mult, ALU.add))
            step(e.tensor_tensor(T3[:, :, :], T3[:, :, :], WDF, ALU.add))
            step(e.tensor_tensor(T3[:, :, :], T3[:, :, :], WSF, ALU.add))
            V["keys"] = st.now
            e.wait_ge(order_in, 32)
            k = E // P
            step(e.memset(over[:, :], 0.0))
            step(e.tensor_tensor(dgt[:, :], dord[:, 0:k], dord[:, 1:k + 1], ALU.is_gt), False)
            step(e.tensor_tensor(dendf[:, 0:TAIL - 1], dend[:, 0:TAIL - 1], dend[:, 1:TAIL], ALU.is_gt))
            step(e.tensor_reduce(over[:, CHK * NB:CHK * NB + 1], dgt[:, :], AX, ALU.add), False)
            step(e.tensor_reduce(over[0:1, CHK * NB + 1:CHK * NB + 2], dendf[:, 0:TAIL - 1], AX, ALU.add), False)
            e.wait_ge(next_in, 32)
            step(e.tensor_tensor(nxt[:, 0:WGRP], nxt[:, 0:WGRP], below[:, 0:WGRP], ALU.subtract), False)
            step(e.tensor_copy(total[0:NB, 0:1], bstart[0:NB, :]))
            step(e.tensor_tensor(nxt[0:NB, WGRP:TCOLS], nxt[0:NB, WGRP:TCOLS], total[0:NB, 0:1], ALU.subtract), False)
            step(e.tensor_scalar(nxt[:, 0:WGRP], nxt[:, 0:WGRP], float(WE), 0.0, ALU.subtract, ALU.max))
            step(e.tensor_scalar(over[0:NB, CHK * NB + 3:CHK * NB + 4], nxt[0:NB, WGRP:TCOLS], float(BE), 0.0, ALU.subtract, ALU.max), False)
            step(e.tensor_reduce(over[:, CHK * NB + 2:CHK * NB + 3], nxt[:, 0:WGRP], AX, ALU.add), False)
            step(e.memset(XN[:, :, :, 0:XW - 1], 0.0), False)
            step(e.memset(XN[:, :, :, XW - 1:XP], 1.0), False)
            e.wait_ge(y_stored, 16)
            e.wait_ge(col_ready, NBAT)
            step(e.memset(pairs[:, 0:4, :], 0.0))
            V["slots"] = st.now

            ohr, owr, taken = Count(oh_ready), Count(ow_ready), Count(h0_taken)
            mvr, x3r = Count(mv_ready), Count(x3_ready)
            aggt, ot, rowr, outr = Count(agg_taken), Count(o_taken), Count(row_ready), Count(out_ready)

            def at(t, j):
                return t[:, bass.ds(j, 1), :].rearrange("p a d -> p (a d)")

            def statistics():
                step(e.bn_stats(lnst[:, :], Z[:, :]))
                settled(e)
                mvr(e.bn_aggr(lnmv[:, :], lnst[:, :]))

            def normed(to, last=None):
                e.wait_ge(sd_ready, mvr.now)
                step(e.reciprocal(lnrs[:, :], lnsd[:, :]))
                ins = e.tensor_scalar(to, Z[:, :], lnmv[:, 0:1], lnrs[:, 0:1], ALU.subtract, ALU.mult)
                mark(last, ins) if last else step(ins)

            def layer_norm(to, last=None):
                statistics()
                normed(to, last)

            def split(v, j):
                row = XN[0:BN, 0, bass.ds(j, 1), :].rearrange("p a d -> p (a d)")
                step(e.tensor_copy(row[:, 0:D], v))
                step(e.tensor_tensor(R[:, :], v, row[:, 0:D], ALU.subtract))
                x3r(e.tensor_scalar(row[:, D:2 * D], R[:, :], LOW, None, ALU.mult))

            dotr, spl = Count(dot_ready), Count(split_ready)
            counts = (st, mvr, x3r, aggt, ot, rowr, outr, spl, taken, ohr, owr, dotr)

            def loop(trips, body, grow):
                with e.Fori(0, trips) as i:
                    for c, n in zip(counts, grow):
                        c.enter(i, n)
                    body(i)
                    for c in counts:
                        c.leave(trips)

            def rows_stats(j, b):
                e.wait_ge(ow_used, LR * (j + 1))
                mark(taken, e.scalar_tensor_tensor(Z[:, :], PS[0:BN, 5 + b, 0:D], ci[:, bass.ds(j, 1)], at(XS, j),
                                                   ALU.mult, ALU.add))
                statistics()

            def rows_done(j):
                normed(at(XS, j))
                split(at(XS, j), j)

            def build_turn(i, first=False):
                for b in range(2):
                    j = 2 * i + b
                    e.wait_ge(ed_in[b], 32 * (i + 1))
                    need(e, ow_ready, LR * (j - 1))
                    step(e.tensor_scalar(dlc[:, b, :], dstc[:, b, :], base[:, bass.ds(j, 1)], None, ALU.subtract), False)
                    step(e.tensor_tensor(ea[:, b, :, :], ea[:, b, :, :], psw[:, :].unsqueeze(1).to_broadcast([P, BT, D]), ALU.mult))
                    dotr(e.tensor_reduce(pac[:, b, :], ea[:, b, :, :], AX, ALU.add))
                    e.wait_ge(cols, COLS * (j + 1))
                    for g in range(GR):
                        n = b * GR + g
                        need(e, win_ready, NBK * (2 * GR * i + n - OR + 1))
                        for w in range(OG):
                            for h in range(WT):
                                t = (n % OR * OG + w) * WT + h
                                W = g * OG + w
                                e.tensor_scalar(KOH[:, t, :], iota_key[:, :], keyc[:, b, h, W:W + 1], None, ALU.is_equal)
                                ins = e.tensor_scalar(LOH[:, t, :], iota_key[:, 0:P], loc[:, b, h, W:W + 1], None, ALU.is_equal)
                        ohr(ins)
                        if g == 1 and not first:
                            rows_done(j - 2)
                    e.wait_ge(sig_ready, j + 1)
                    for g in range(LR):
                        n = b * LR + g
                        need(e, ow_used, 2 * LR * i + n - OR + 1)
                        for q in range(min(LG, BT - g * LG)):
                            t = g * LG + q
                            ins = e.tensor_scalar(OHW[:, (n % OR) * LG + q, :], iota_f[:, 0:BN], dlc[:, b, t:t + 1],
                                                  pac[:, b, t:t + 1], ALU.is_equal, ALU.mult)
                        owr(ins)
                        if g == 1 and not (first and b == 0):
                            rows_stats(j - 1, 1 - b)

            build_turn.grow = (2 * 7, 2, 2, 0, 0, 0, 0, 0, 2, 2 * GR, 2 * LR, 2)
            build_turn(0, True)
            loop(NB // 2 - 1, lambda i: build_turn(i + 1), build_turn.grow)
            rows_done(NB - 2)
            rows_stats(NB - 1, 1)
            rows_done(NB - 1)
            step(e.memset(XH[:, :, :], 0.0))
            e.wait_ge(ed_in[0], 32 * (NB // 2 + 1))
            e.wait_ge(src_in[0], 16 * (NB // 2 + 1))

            e.wait_ge(over_kept, NB)
            step(e.memset(total[:, 1:2], 1.0))
            e.tensor_reduce(total[:, 0:1], over[:, :], AX, ALU.add).then_inc(total_ready, 1)
            e.wait_ge(total_sum, 1)
            e.tensor_scalar(slow[:, :], PS[0:1, 7, 0:1], 0.0, None, ALU.is_gt).then_inc(slow_ready, 1)
            e.wait_ge(slow_ready, 1)
            general = e.value_load(slow[0:1, 0:1], min_val=0, max_val=1)

            gs = Count(gz["step"])

            def gstep(ins):
                e.wait_ge(gz["step"], gs(ins))
                settled(e)

            def general_sums(c, swap, count):
                gstep(e.memset(g_msg[:, :], 0.0))
                gstep(e.memset(GA[:, :, :], 0.0))
                e.sem_inc(gz["start"], 1)
                with e.Fori(0, NT) as t:
                    gs.enter(t, 12 if c == 0 else 10)
                    n = NT * c + t + 1
                    e.wait_ge(gz_in[c], 48 * (t + 1))
                    if c == 0:
                        e.wait_ge(gz["edge"], 16 * (t + 1))
                    settled(e)
                    gstep(e.tensor_copy(g_farf[:, :], g_far[:, :]))
                    gstep(e.tensor_copy(g_nearf[:, :], g_near[:, :]))
                    gstep(e.tensor_copy(g_rowf[:, :], g_row[:, :]))
                    gstep(e.tensor_scalar(g_c[:, 0:1], (g_farf if swap else g_nearf)[:, :], N - 0.5, None, ALU.is_lt))
                    gstep(e.tensor_scalar(g_idx[:, 0:1], g_farf[:, :], N - 1.0, None, ALU.min))
                    gstep(e.tensor_scalar(g_idx[:, 1:2], g_nearf[:, :], N - 1.0, None, ALU.min))
                    gstep(e.tensor_scalar(g_same[:, :], g_rowf[:, :], g_nearf[:, 0:1], None, ALU.is_equal))
                    gstep(e.tensor_tensor(g_tmp[:, :], g_same[:, :], g_before[:, :], ALU.mult))
                    gstep(e.tensor_reduce(g_c[:, 1:2], g_tmp[:, :], AX, ALU.add))
                    e.scalar_tensor_tensor(g_idx[:, 2:3], g_c[:, 1:2], DUP, g_nearf[:, :], ALU.mult, ALU.add).then_inc(gz["index"], 1)
                    if c == 0:
                        gstep(e.tensor_tensor(g_edge[:, :], g_edge[:, :], psw[:, :], ALU.mult))
                        e.tensor_reduce(g_c[:, 2:3], g_edge[:, :], AX, ALU.add).then_inc(gz["dot"], 1)
                        e.wait_ge(gz["sig"], t + 1)
                        settled(e)
                        gstep(e.tensor_tensor(g_c[:, 3:4], g_c[:, 2:3], g_c[:, 0:1], ALU.mult))
                    weight = g_c[:, 3:4] if c == 0 else g_c[:, 0:1]
                    if count:
                        gstep(e.tensor_copy(g_msg[:, 2 * D:2 * D + 1], g_c[:, 0:1]))
                    else:
                        gstep(e.memset(g_msg[:, 2 * D:2 * D + 1], 0.0))
                    e.wait_ge(gz_rows[c], 32 * (t + 1))
                    settled(e)
                    e.tensor_scalar(g_msg[:, 0:D], g_got[:, :], weight, None, ALU.mult).then_inc(gz["msg"], 1)
                    e.wait_ge(gz["sum"], n)
                    settled(e)
                    e.tensor_tensor(g_acc[:, :], g_acc[:, :], PS[:, 6, 0:HW], ALU.add).then_inc(gz["added"], 1)
                    e.wait_ge(gz["added"], n)
                    gs.leave(NT)

            with e.If(general > 0):
                general_sums(0, False, False)
                with e.Fori(0, NB) as j:
                    gs.enter(j, 4)
                    e.wait_ge(gz["block_in"], 16 * (j + 1))
                    settled(e)
                    gstep(e.scalar_tensor_tensor(Z[:, :], GA[:, 0, 0:D], ci[:, bass.ds(j, 1)], at(XS, j), ALU.mult, ALU.add))
                    gstep(e.bn_stats(lnst[:, :], Z[:, :]))
                    settled(e)
                    e.bn_aggr(lnmv[:, :], lnst[:, :]).then_inc(gz["mv"], 1)
                    e.wait_ge(gz["sd"], j + 1)
                    settled(e)
                    gstep(e.reciprocal(lnrs[:, :], lnsd[:, :]))
                    gstep(e.tensor_scalar(at(XS, j), Z[:, :], lnmv[:, 0:1], lnrs[:, 0:1], ALU.subtract, ALU.mult))
                    e.sem_inc(gz["x1"], 1)
                    gs.leave(NB)

            def gather_in(p, j, u):
                inv = AG[:, D + 1:D + 2] if p == 3 else RC[:, bass.ds(j, 1)]
                if p in (0, 3):
                    step(e.tensor_scalar(AG[:, D:D + 1], PS[0:BN, u, 2 * D:XW], 1.0, None, ALU.max))
                    step(e.reciprocal(inv, AG[:, D:D + 1]))
                high = PS[0:BN, u, 0:D]
                if p == 1:
                    step(e.tensor_copy(MX[:, u, D:2 * D], at(HS, j)), False)
                    mark(aggt, e.tensor_reduce(AG[:, 0:D], PS[0:BN, u, 0:HW].rearrange("p (q d) -> p d q", d=D), AX, ALU.add))
                    mark(rowr, e.tensor_scalar(MX[:, u, 0:D], AG[:, 0:D], inv, None, ALU.mult))
                    return
                if p == 4:
                    step(e.scalar_tensor_tensor(AG[:, 0:D], at(XS, j), ope[0:BN, 0:1], high, ALU.mult, ALU.add))
                    mark(aggt, e.scalar_tensor_tensor(MX[:, u, 0:D], PS[0:BN, u, D:2 * D], 1.0 / LOW, AG[:, 0:D], ALU.mult, ALU.add))
                    return
                step(e.tensor_scalar(AG[:, 0:D], PS[0:BN, u, D:2 * D], inv, 1.0 / LOW, ALU.mult, ALU.mult))
                if p == 0:
                    step(e.tensor_copy(MX[:, u, D:2 * D], at(XS, j)), False)
                    to = MX[:, u, 0:D]
                elif p == 2:
                    to = at(HS, j)
                else:
                    step(e.tensor_copy(MX[:, u, 0:D], at(HS, j)), False)
                    step(e.tensor_copy(MX[:, u, D:2 * D], at(XS, j)), False)
                    to = MO[:, u, :]
                mark(aggt, e.scalar_tensor_tensor(to, high, inv, AG[:, 0:D], ALU.mult, ALU.add))

            def finish(p, j):
                n = {0: 0, 1: 1, 3: 2, 4: 5}[p]
                mark(ot, e.tensor_tensor(Z[:, :], PS[0:BN, 7, 0:D], bias[0:BN, n, :], ALU.add))
                if p == 0:
                    mark(spl, e.tensor_scalar(at(HS, j), Z[:, :], 0.0, None, ALU.max))
                    return
                step(e.tensor_tensor(Z[:, :], Z[:, :], at(XS, j), ALU.add))
                layer_norm(at(XS if p < 4 else OUTS, j), outr if p == 4 else spl)

            GROW = {0: (4, 0, 0, 1, 1, 0, 0, 1), 1: (1 + 3, 1, 0, 1, 1, 1, 0, 1), 2: (1, 0, 0, 1, 0, 0, 0, 0),
                    3: (5 + 3, 1, 0, 1, 1, 0, 0, 1), 4: (1 + 3, 1, 0, 1, 1, 0, 1, 0)}
            for p in range(5):
                def turn(g, gather, fin, p=p):
                    for u in range(RING):
                        if gather and p != 3:
                            e.wait_ge(slot_used[u], NG * p + g + 1)
                            gather_in(p, RING * g + u, u)
                        if fin:
                            j = RING * (g - 1) + u
                            e.wait_ge(o_ready, NB * F_OF[p] + j + 1)
                            finish(p, j)
                    if gather and p == 3:
                        e.wait_ge(slot_used[RING - 1], NG * p + g + 1)
                        for u in range(RING):
                            gather_in(p, RING * g + u, u)

                with e.If(general > 0):
                    general_sums(p + 1, p == 3, p in (0, 3))
                turn(0, True, False)
                loop(NG - 1, lambda i: turn(i + 1, True, p != 2), tuple(RING * n for n in GROW[p]) + (0,) * 4)
                if p != 2:
                    turn(NG, False, True)

        @block.gpsimd
        def _(e):
            e.iota(iota_i[:, :], pattern=[[1, KW]], base=0, channel_multiplier=0)
            e.iota(base_i[:, :], pattern=[[BN, NB]], base=0, channel_multiplier=0)
            e.iota(thr_i[:, 0:WGRP], pattern=[[WN * P, WGRP]], base=0, channel_multiplier=WN)
            e.iota(thr_i[:, WGRP:TCOLS], pattern=[[0, 1]], base=0, channel_multiplier=BN)
            e.memset(lowt[:, :], LOW)
            e.memset(ident_f[:, :], 0.0).then_inc(iota_done, 1)
            e.wait_ge(iota_done, 1)
            e.affine_select(out=ident_f[:, :], in_=ident_f[:, :], compare_op=ALU.not_equal, fill=1.0,
                            base=0, pattern=[[-1, P]], channel_multiplier=1).then_inc(iota_done, 1)

            def gather(to, table, index, axis, s):
                e.indirect_dma_start(out=to, out_offset=None, in_=table,
                                     in_offset=bass.IndirectOffsetOnAxis(ap=index, axis=axis)).then_inc(s, 16)

            e.wait_ge(dve_step, V["rows"])
            for g in range(TCOLS):
                gather(low_i[:, g, :], dst_rows, rowi[:, g:g + 1], 0, low_in)
            e.wait_ge(dve_step, V["starts"])
            for g in range(WGRP):
                gather(WD[:, g, :], dst_flat, starts[:, g:g + 1], 1, win_in)
                gather(WS[:, g, :], src_flat, starts[:, g:g + 1], 1, win_in)
            e.wait_ge(y_stored, 16)

            def rows_turn(i):
                for b in range(2):
                    e.wait_ge(src_in[b], 16 * (i + 1))
                    need(e, ow_used, LR * (2 * i + b - 1))
                    settled(e)
                    for t in range(BT):
                        gather(G[:, b, t, :], y_dram, srcc[:, b, t:t + 1], 0, rows_in[b])

            rows_turn(0)
            with e.Fori(0, NB // 2 - 1) as i:
                rows_turn(i + 1)

            e.wait_ge(slow_ready, 1)
            general = e.value_load(slow[0:1, 0:1], min_val=0, max_val=1)

            def general_sums(c):
                e.wait_ge(gz["start"], c + 1)
                e.wait_ge(gz["prep"], 16 * sum(PREPS[:c + 1]))
                e.sem_inc(gz["next"], 1)
                table = y_dram if c == 0 else row_dram
                with e.Fori(0, NT) as t:
                    n = NT * c + t + 1
                    e.wait_ge(gz["index"], n)
                    settled(e)
                    gather(g_got[:, :], table, g_idx[:, 0:1], 0, gz_rows[c])
                    gather(g_acc[:, :], sum_dram, g_idx[:, 1:2], 0, gz_rows[c])
                    e.wait_ge(gz["added"], n)
                    settled(e)
                    e.indirect_dma_start(out=sum_dram, out_offset=bass.IndirectOffsetOnAxis(ap=g_idx[:, 2:3], axis=0),
                                         in_=g_acc[:, :], in_offset=None, bounds_check=N - 1, oob_is_err=False).then_inc(gz_kept[c], 16)
                    e.wait_ge(gz_kept[c], 16 * (t + 1))
                    e.sem_inc(gz["next"], 1)

            with e.If(general > 0):
                e.memset(g_before[:, :], 1.0).then_inc(gz["mask"], 1)
                e.wait_ge(gz["mask"], 1)
                e.affine_select(out=g_before[:, :], in_=g_before[:, :], compare_op=ALU.is_gt, fill=0.0,
                                base=0, pattern=[[-1, P]], channel_multiplier=1).then_inc(gz["mask"], 1)
                e.wait_ge(gz["mask"], 2)
                general_sums(0)
            st, x3r = Count(pool_step), Count(x3_ready)
            for f, p in enumerate((0, 1, 3)):
                with e.If(general > 0):
                    if p == 3:
                        general_sums(3)
                    general_sums(p + 1)
                with e.Fori(0, NB) as j:
                    st.enter(j, 3 if p == 0 else 2)
                    e.wait_ge(split_ready, NB * f + j + 1)
                    settled(e)
                    here = bass.ds(j, 1)
                    v = (HS if p == 0 else XS)[:, here, :].rearrange("p a d -> p (a d)")
                    to = (XH[0:BN, here, :] if p == 0 else XN[0:BN, 0 if p == 1 else 1, here, :]).rearrange("p a d -> p (a d)")

                    def step(ins):
                        e.wait_ge(pool_step, st(ins))
                        settled(e)

                    step(e.tensor_copy(to[:, 0:D], v))
                    step(e.tensor_tensor(RP[:, :], v, to[:, 0:D], ALU.subtract))
                    if p == 0:
                        step(e.tensor_copy(to[:, D:2 * D], RP[:, :]))
                        x3r(e.tensor_tensor(to[:, 2 * D:HW], RP[:, :], to[:, D:2 * D], ALU.subtract))
                    else:
                        x3r(e.tensor_tensor(to[:, D:2 * D], RP[:, :], lowt[:, :], ALU.mult))
                    e.wait_ge(x3_ready, NB * (f + 1) + j + 1)
                    st.leave(NB)
            with e.If(general > 0):
                general_sums(5)
            outv = out.rearrange("(b p) d -> p b d", p=BN)
            with e.Fori(0, NG) as g:
                e.wait_ge(out_ready, RING * (g + 1))
                e.dma_start(outv[:, bass.ds(RING * g, RING), :], OUTS[:, bass.ds(RING * g, RING), :]).then_inc(out_stored, 16)
            e.wait_ge(out_stored, 16 * NG)

        @block.sync
        def _(e):
            e.dma_start(samp_i, samples.rearrange("(a s) -> a s", a=1).to_broadcast([P, SAMP])).then_inc(in_samp, 16)
            e.dma_start(XS[:, :, :], x_t).then_inc(in_x, 16)
            e.dma_start(cj[:, :], cj_t).then_inc(in_x, 16)
            e.dma_start(ci[:, :], ci_t).then_inc(in_x, 16)
            e.dma_start(psw[:, :], ps_w.to_broadcast([P, D])).then_inc(in_w, 16)
            with nc.allow_non_contiguous_dma(reason="a bias as a column"):
                for to, frm in ((W1[:, :], w1), (W2[:, :], w2), (W3[:, :], w3), (W3o[:, :], w3o), (W4a[:, :], w4a),
                                (W4b[:, :, :], w4b.rearrange("(c k) n -> k c n", c=2)),
                                (b4[:, :], b4a.rearrange("(c k) -> k c", c=2))):
                    e.dma_start(to, frm).then_inc(in_w, 16)
            for n, v in enumerate((b1, b2, b3s, b3i, b3o, b4b)):
                e.dma_start(bias[:, n, :], v.rearrange("(a d) -> a d", a=1).to_broadcast([P, D])).then_inc(in_w, 16)
            e.dma_start(ope[:, :], eps.rearrange("(a d) -> a d", a=1).to_broadcast([P, 1])).then_inc(in_w, 16)
            k = E // P
            ordered = bass.AP(tensor=dst.tensor, offset=0, ap=[[k, P], [1, k + 1]])
            e.dma_start(dord[:, :], ordered).then_inc(order_in, 16)
            e.dma_start(dend[:, :], dst[k * P:E].rearrange("(a n) -> a n", a=1)).then_inc(order_in, 16)
            e.wait_ge(dve_step, V["y"])
            e.dma_start(y_dram.rearrange("(b p) d -> p b d", p=BN), ytile[:, :, :]).then_inc(y_stored, 16)
            e.wait_ge(dve_step, V["starts"])
            e.dma_start(bst_dram, bstart[0:NB + 2, :]).then_inc(bst_stored, 16)
            e.wait_ge(bst_stored, 16)

            def load_edges(i, b):
                j = 2 * i + b
                need(e, rows_in[b], 16 * BT * i)
                settled(e)
                first = e.value_load(bst_dram[bass.ds(j, 1), :], min_val=0, max_val=E - BE)
                e.dma_start(srcc[:, b, :], src[bass.ds(first, BE)].rearrange("(p t) -> p t", t=BT)).then_inc(src_in[b], 16)
                need(e, ow_used, LR * (j - 1))
                e.dma_start(dstc[:, b, :], dst[bass.ds(first, BE)].rearrange("(p t) -> p t", t=BT)).then_inc(ed_in[b], 16)
                e.dma_start(ea[:, b, :, :], edge_attr[bass.ds(first, BE), :].rearrange("(p t) d -> p t d", t=BT)).then_inc(ed_in[b], 16)

            def store_turn(i):
                for b in range(2):
                    j = 2 * i + b
                    load_edges(i + b, 1 - b)
                    e.wait_ge(win_out, WOUT * (j + 1))
                    e.dma_start(at_dram[bass.ds(j, 1), :, :].rearrange("a p n -> (a p) n"), pairs[:, b, :]).then_inc(at_stored[b], 16)
                    e.wait_ge(tr_out, TROUT * (j + 1))
                    e.dma_start(a_dram[bass.ds(j, 1), :, :].rearrange("a p n -> (a p) n"), pairs[:, 2 + b, :]).then_inc(a_stored[b], 16)

            load_edges(0, 0)
            with nc.allow_non_contiguous_dma(reason="starts in the order of the windows"):
                e.dma_start(wst_dram[0:WGRP * P, :].rearrange("(g p) a -> p (g a)", p=P), below[:, 0:WGRP]).then_inc(wst_stored, 16)
                e.dma_start(wst_dram[WGRP * P:WGRP * P + 1, :], below[P - 1:P, WGRP - 1:WGRP]).then_inc(wst_stored, 16)
                e.wait_ge(wst_stored, 32)
                e.dma_start(nxt[:, 0:WGRP], wst_dram[1:WGRP * P + 1, :].rearrange("(g p) a -> p (g a)", p=P)).then_inc(next_in, 16)
                e.dma_start(nxt[0:NB, WGRP:TCOLS], wst_dram[WB:WB * (NB + 1), :].rearrange("(p w) a -> p (w a)", w=WB)[:, 0:1]).then_inc(next_in, 16)
            store_turn(0)
            with e.Fori(0, NB // 2 - 1) as i:
                store_turn(i + 1)
            for s in (*at_stored, *a_stored):
                e.wait_ge(s, 16 * (NB // 2))
            e.wait_ge(checked, CHK * NB)

            def load_turn(p, g):
                for u in range(RING):
                    need(e, slot_used[u], g + NG * p)
                    if p == 3:
                        rows = NB // RING
                        w = RING * PITCH // 2
                        to = pairs[:, u, :].rearrange("p (j n) -> p j n", n=w)
                        frm = a_dram[rows * u:rows * (u + 1), :, bass.ds(g * w, w)].rearrange("j p n -> p j n")
                    else:
                        to = pairs[:, u, :]
                        frm = at_dram[bass.ds(RING * g + u, 1), :, :].rearrange("a p n -> (a p) n")
                    e.dma_start(to, frm).then_inc(slot_in[u], 16)

            def general_sums(c, near, far):
                e.wait_ge(gz["start"], c + 1)
                for k in range(NG):
                    e.dma_start(sum_dram[k * RING * BN:(k + 1) * RING * BN, :].rearrange("(b p) d -> p b d", p=BN), GA[:, :, :]).then_inc(gz["prep"], 16)
                if c > 0:
                    rows = HS if c == 2 else XS
                    e.dma_start(row_dram.rearrange("(b p) d -> p b d", p=BN), rows[:, :, :]).then_inc(gz["prep"], 16)
                e.wait_ge(gz["prep"], 16 * sum(PREPS[:c + 1]))
                def edges(t, rows):
                    e.wait_ge(gz["next"], (NT + 1) * c + t + 1)
                    at = bass.ds(t * P, P)
                    e.dma_start(g_far[:, :], far[at].rearrange("(p a) -> p a", a=1)).then_inc(gz_in[c], 16)
                    e.dma_start(g_near[:, :], near[at].rearrange("(p a) -> p a", a=1)).then_inc(gz_in[c], 16)
                    e.dma_start(g_row[:, :], near[at].rearrange("(a p) -> a p", a=1).to_broadcast([P, P])).then_inc(gz_in[c], 16)
                    if c == 0:
                        e.dma_start(g_edge[0:rows, :], edge_attr[bass.ds(t * P, rows), :]).then_inc(gz["edge"], 16)

                with e.Fori(0, NT - 1) as t:
                    edges(t, P)
                edges(NT - 1, E - (NT - 1) * P)
                e.wait_ge(gz["next"], (NT + 1) * (c + 1))

            e.wait_ge(slow_ready, 1)
            general = e.value_load(slow[0:1, 0:1], min_val=0, max_val=1)
            with e.If(general > 0):
                e.dma_start(XS[:, :, :], x_t).then_inc(gz["prep"], 16)
                general_sums(0, dst, src)
                e.dma_start(GA[:, 0, :], sum_dram[0:BN, :]).then_inc(gz["block_in"], 16)
                with e.Fori(1, NB) as j:
                    e.wait_ge(gz["x1"], j)
                    e.dma_start(GA[:, 0, :], sum_dram[bass.ds(j * BN, BN), :]).then_inc(gz["block_in"], 16)
                e.wait_ge(gz["x1"], NB)
            for p in range(5):
                with e.If(general > 0):
                    if p > 0:
                        e.wait_ge(x3_ready, X_NEED[p])
                    general_sums(p + 1, *((src, dst) if p == 3 else (dst, src)))

                    def sums_turn(g):
                        for u in range(RING):
                            need(e, slot_used[u], g + NG * p)
                            e.dma_start(GA[:, u, :], sum_dram[bass.ds((RING * g + u) * BN, BN), :]).then_inc(slot_in[u], 16)

                    sums_turn(0)
                    with e.Fori(1, NG) as g:
                        sums_turn(g)
                with e.Else():
                    load_turn(p, 0)
                    with e.Fori(0, NG - 1) as g:
                        load_turn(p, g + 1)

        @block.scalar
        def _(e):
            for n, (a, h, items) in enumerate(batches):
                e.wait_ge(col_ready, n + 1)
                to = (KEYT, LOT)[a][:, h, items[0] * P:(items[-1] + 1) * P]
                e.activation(to, PS[:, n % 2, 0:len(items) * P], ACT.Copy).then_inc(col_out, 1)
            e.wait_ge(col_out, NBAT)
            e.wait_ge(dve_step, V["slots"])

            def windows(j, b):
                need(e, oh_ready, GR * (j - 1))
                window = bass.ds(j * WB, WB)
                e.activation(keyc[:, b, :, :], KEYT[:, :, window], ACT.Copy).then_inc(cols, 1)
                e.activation(loc[:, b, :, :], LOT[:, :, window], ACT.Copy).then_inc(cols, 1)

            def deviation(j):
                e.wait_ge(mv_ready, j + 1)
                e.activation(lnsd[:, :], lnmv[:, 1:2], ACT.Sqrt, bias=epsc[0:BN, 0:1]).then_inc(sd_ready, 1)

            def build_turn(i, first=False):
                for b in range(2):
                    j = 2 * i + b
                    windows(j + 1, 1 - b)
                    e.wait_ge(dot_ready, j + 1)
                    e.activation(pac[:, b, :], pac[:, b, :], ACT.Sigmoid).then_inc(sig_ready, 1)
                    need(e, at_stored[b], 16 * i)
                    need(e, over_kept, j - 1)
                    slot = slots[:, b, :].rearrange("p (h c) -> p h c", c=PITCH)[:, :, 0:BN].rearrange("p h (w l) -> p w h l", l=WN)
                    for g in range(GR):
                        for k, ws in enumerate(BANKS):
                            e.wait_ge(win_ready, WOUT * j + NBK * g + k + 1)
                            w = OG * g + ws[0]
                            settled(e)
                            e.activation(slot[:, w:w + len(ws), :, :],
                                         PS[:, k, 0:len(ws) * KW].rearrange("p (w h l) -> p w h l", h=NB, l=WN),
                                         ACT.Copy, saturate=False).then_inc(win_out, 1)
                    need(e, a_stored[b], 16 * i)
                    slot = slots[0:BN, 2 + b, :].rearrange("p (h c) -> p h c", c=PITCH)
                    for n in range(TROUT):
                        h0, h1 = TB * n, min(TB * n + TB, NB)
                        e.wait_ge(tr_ready, TROUT * j + n + 1)
                        bank = PS[0:BN, 3 + (b * TROUT + n) % 2, :].rearrange("p (h c) -> p h c", c=PITCH)
                        settled(e)
                        e.activation(slot[:, h0:h1, :], bank[:, 0:h1 - h0, :], ACT.Copy, saturate=False).then_inc(tr_out, 1)
                        if n == TSPLIT[2] - 1 and not (first and b == 0):
                            deviation(j - 1)
                        if n + 1 in TSPLIT:
                            k = TSPLIT.index(n + 1) - 1
                            cw = NB * PITCH // CHK
                            need(e, checked, CHK * (j - 1) + k + 1)
                            settled(e)
                            e.activation(junk[:, k * cw:(k + 1) * cw], slots[:, b, k * cw:(k + 1) * cw], ACT.Relu, bias=most[:, 0:1],
                                         saturate=False, accum_out=overc[:, b, k:k + 1]).then_inc(checked, 1)
                    e.wait_ge(checked, CHK * (j + 1))
                    e.activation(over[:, bass.ds(j * CHK, CHK)], overc[:, b, :], ACT.Copy).then_inc(over_kept, 1)

            windows(0, 0)
            build_turn(0, True)
            with e.Fori(0, NB // 2 - 1) as i:
                build_turn(i + 1)
            deviation(NB - 1)
            e.wait_ge(slow_ready, 1)
            general = e.value_load(slow[0:1, 0:1], min_val=0, max_val=1)
            with e.If(general > 0):
                with e.Fori(0, NT) as t:
                    e.wait_ge(gz["dot"], t + 1)
                    e.activation(g_c[:, 2:3], g_c[:, 2:3], ACT.Sigmoid).then_inc(gz["sig"], 1)
                with e.Fori(0, NB) as j:
                    e.wait_ge(gz["mv"], j + 1)
                    e.activation(lnsd[:, :], lnmv[:, 1:2], ACT.Sqrt, bias=epsc[0:BN, 0:1]).then_inc(gz["sd"], 1)
            for p in (0, 1, 3, 4):
                with e.Fori(0, NG) as g:
                    for u in range(RING):
                        j = RING * g + u
                        e.wait_ge(mt_ready, NB * F_OF[p] + j + 1)
                        k = D if p == 4 else P
                        e.activation(TS[0:k, 0, 0:BN], PS[0:k, 5, 0:BN], ACT.Copy).then_inc(ts_ready, 1)
                        if p == 3:
                            e.activation(TS[0:D, 1, 0:BN], PS[0:D, 5, P:P + BN], ACT.Copy).then_inc(ts_ready, 1)
                        if p == 4:
                            e.wait_ge(h1_ready, j + 1)
                            for c in range(2):
                                e.activation(H1[:, c, :], PS[:, 6, c * P:c * P + BN], ACT.Identity, bias=b4[:, c:c + 1]).then_inc(h1_out, 1)
                        if p != 0:
                            e.wait_ge(mv_ready, NORM0[p] + j + 1)
                            e.activation(lnsd[:, :], lnmv[:, 1:2], ACT.Sqrt, bias=epsc[0:BN, 0:1]).then_inc(sd_ready, 1)

        @block.tensor
        def _(e):
            e.wait_ge(dve_step, V["keys"])
            for n, (a, h, items) in enumerate(batches):
                if n >= 2:
                    e.wait_ge(col_out, n - 1)
                for k, it in enumerate(items):
                    frm = (T3, T1)[a][:, it, h * P:(h + 1) * P]
                    ins = e.transpose(PS[:, n % 2, k * P:(k + 1) * P], frm, ident_f[:, :])
                ins.then_inc(col_ready, 1)
            e.wait_ge(col_out, NBAT)

            def build_turn(i):
                for b in range(2):
                    j = 2 * i + b
                    for g in range(GR):
                        n = b * GR + g
                        e.wait_ge(oh_ready, GR * j + g + 1)
                        for k, ws in enumerate(BANKS):
                            need(e, win_out, WOUT * j + NBK * (g - 1) + k + 1)
                            for q, w in enumerate(ws):
                                for h in range(WT):
                                    t = (n % OR * OG + w) * WT + h
                                    ins = e.matmul(PS[:, k, q * KW:(q + 1) * KW], LOH[:, t, :], KOH[:, t, :], start=h == 0, stop=h == WT - 1)
                            ins.then_inc(win_ready, 1)
                    need(e, h0_taken, j - 1)
                    e.wait_ge(rows_in[b], 16 * BT * (i + 1))
                    for g in range(LR):
                        e.wait_ge(ow_ready, LR * j + g + 1)
                        for q in range(min(LG, BT - g * LG)):
                            t = g * LG + q
                            ins = e.matmul(PS[0:BN, 5 + b, 0:D], OHW[:, ((b * LR + g) % OR) * LG + q, :], G[:, b, t, :],
                                           start=t == 0, stop=t == BT - 1)
                        ins.then_inc(ow_used, 1)
                        e.wait_ge(win_out, WOUT * (j + 1))
                        for n in range(*TSPLIT[g:g + 2]):
                            need(e, tr_out, TROUT * j + n - 1)
                            settled(e)
                            bank = PS[:, 3 + (b * TROUT + n) % 2, :]
                            for k, h in enumerate(range(TB * n, min(TB * n + TB, NB))):
                                ins = e.matmul(bank[:, k * PITCH:(k + 1) * PITCH], slots[:, b, h * PITCH:(h + 1) * PITCH], ident_b[:, :],
                                               start=True, stop=True)
                            ins.then_inc(tr_ready, 1)

            build_turn(0)
            with e.Fori(0, NB // 2 - 1) as i:
                build_turn(i + 1)

            e.wait_ge(total_ready, 1)
            e.matmul(PS[0:1, 7, 0:1], total[:, 0:1], total[:, 1:2], start=True, stop=True).then_inc(total_sum, 1)
            e.wait_ge(slow_ready, 1)
            general = e.value_load(slow[0:1, 0:1], min_val=0, max_val=1)

            def general_sums(c):
                with e.Fori(0, NT) as t:
                    e.wait_ge(gz["msg"], NT * c + t + 1)
                    e.matmul(PS[:, 6, 0:HW], g_same[:, :], g_msg[:, :], start=True, stop=True).then_inc(gz["sum"], 1)

            with e.If(general > 0):
                general_sums(0)

            for p in range(5):
                x3 = X_IN[p]
                wide = {0: XW, 1: HW, 2: 2 * D, 3: XW, 4: 2 * D}[p]

                def turn(g, gather, fin, fast, p=p, x3=x3, wide=wide):
                    for u in range(RING):
                        if fin:
                            f = F_OF[p]
                            j = RING * (g - 1) + u
                            ts = 2 if p == 3 else 1
                            if p == 1:
                                e.wait_ge(row_ready, j + 1)
                            else:
                                e.wait_ge(agg_taken, NB * p + j + 1)
                            need(e, ts_ready, TS0[p] + ts * j)
                            if p == 4:
                                settled(e)
                                e.transpose(PS[0:D, 5, 0:BN], MX[:, u, 0:D], ident_f[0:BN, 0:BN]).then_inc(mt_ready, 1)
                            else:
                                ins = e.transpose(PS[:, 5, 0:BN], MX[:, u, :], ident_f[0:BN, 0:BN])
                                if p == 3:
                                    ins = e.transpose(PS[0:D, 5, P:P + BN], MO[:, u, :], ident_f[0:BN, 0:BN])
                                ins.then_inc(mt_ready, 1)
                        if gather:
                            e.wait_ge(slot_in[u], 16 * (NG * p + g + 1))
                            if p == 3:
                                if u == 0:
                                    e.wait_ge(agg_taken, NB * p + RING * g)
                            else:
                                need(e, agg_taken, NB * p + RING * g + u - RING + 1)

                            settled(e)

                        def products(a, b):
                            if not fast:
                                if b == NB:
                                    e.matmul(PS[0:BN, u, 0:wide], ident_f[0:BN, 0:BN], GA[:, u, 0:wide], start=True, stop=True).then_inc(slot_used[u], 1)
                                return
                            for n in range(a, b):
                                if p == 3:
                                    k, q = n // RING, n % RING
                                    m = e.matmul(PS[:, q, 0:wide], slots[:, u, n * PITCH:(n + 1) * PITCH], x3[:, u * (NB // RING) + k, 0:wide],
                                                 start=u == 0 and k == 0, stop=u == RING - 1 and k == NB // RING - 1)
                                else:
                                    m = e.matmul(PS[:, u, 0:wide], slots[:, u, n * PITCH:(n + 1) * PITCH], x3[:, n, 0:wide],
                                                 start=n == 0, stop=n == NB - 1)
                            if b == NB:
                                m.then_inc(slot_used[u], 1)

                        if gather:
                            products(0, NB // 2)
                        if fin and p == 4:
                            e.wait_ge(ts_ready, TS0[p] + j + 1)
                            need(e, h1_out, 2 * j)
                            for c in range(2):
                                ins = e.matmul(PS[:, 6, c * P:c * P + BN], W4a[:, c * P:(c + 1) * P], TS[0:D, 0, 0:BN], start=True, stop=True)
                            ins.then_inc(h1_ready, 1)
                        if gather:
                            products(NB // 2, NB)
                        if fin:
                            need(e, o_taken, NB * f + j)
                            o = PS[0:BN, 7, 0:D]
                            if p == 4:
                                e.wait_ge(h1_out, 2 * (j + 1))
                                e.matmul(o, H1[:, 0, :], W4b[:, 0, :], start=True, stop=False)
                                ins = e.matmul(o, H1[:, 1, :], W4b[:, 1, :], start=False, stop=True)
                            else:
                                e.wait_ge(ts_ready, TS0[p] + ts * (j + 1))
                                W = (W1, W2, None, W3)[p]
                                ins = e.matmul(o, TS[:, 0, 0:BN], W[:, :], start=True, stop=p != 3)
                                if p == 3:
                                    ins = e.matmul(o, TS[0:D, 1, 0:BN], W3o[:, :], start=False, stop=True)
                            ins.then_inc(o_ready, 1)

                e.wait_ge(x3_ready, X_NEED[p])

                def turns(fast, p=p, turn=turn):
                    turn(0, True, False, fast)
                    turn(1, True, p != 2, fast)
                    with e.Fori(0, NG - 2) as i:
                        turn(i + 2, True, p != 2, fast)
                    if p != 2:
                        turn(NG, False, True, fast)

                with e.If(general > 0):
                    general_sums(p + 1)
                    turns(False)
                with e.Else():
                    turns(True)


def kernel(**inputs):
    import concourse.bacc as bacc
    import numpy as np
    from concourse.bass_utils import run_bass_kernel_spmd

    v = {k: np.asarray(a) for k, a in inputs.items()}

    def nodes(a):
        return np.ascontiguousarray(a.reshape(NB, BN, -1).transpose(1, 0, 2))

    def padded(a, fill):
        return np.concatenate([a, np.full(EP - E, fill, a.dtype)])

    arrays = {
        "x_t": nodes(v["x"]),
        "cj_t": nodes(v["node_vec1"])[:, :, 0],
        "ci_t": nodes(v["node_vec1_n2"])[:, :, 0],
        "src_p": padded(v["src"], 0),
        "dst_p": padded(v["dst"], 2 * N),
        "samples": v["dst"][::P],
        "edge_attr": v["edge_attr_64"],
        "ps_w": v["L0_gnn_ps_w"],
        "w1": np.concatenate([v["L1_gnn_W1_l"].T, v["L1_gnn_W1_r"].T]),
        "b1": v["L1_gnn_b1"],
        "w2": np.concatenate([v["L1_gnn_W2_l"].T, v["L1_gnn_W2_r"].T]),
        "b2": v["L1_gnn_b2"],
        "w3": np.concatenate([v["L2_gnn_W_s2d"], v["L2_gnn_W_self"]]),
        "w3o": v["L2_gnn_W_d2s"],
        "b3s": v["L2_gnn_b_self"],
        "b3i": v["L2_gnn_b_s2d"],
        "b3o": v["L2_gnn_b_d2s"],
        "w4a": v["L3_gnn_W1"],
        "b4a": v["L3_gnn_b1"],
        "w4b": v["L3_gnn_W2"],
        "b4b": v["L3_gnn_b2"],
        "eps": v["L3_gnn_eps"],
    }
    arrays = {k: np.ascontiguousarray(a) for k, a in arrays.items()}
    nc = bacc.Bacc("TRN2", target_bir_lowering=False, num_devices=1)
    args = [nc.dram_tensor(k, a.shape, mybir.dt.from_np(a.dtype), kind="ExternalInput").ap() for k, a in arrays.items()]
    args.append(nc.dram_tensor("out", (N, D), F32, kind="ExternalOutput").ap())
    build(nc, *args)
    return run_bass_kernel_spmd(nc, [arrays], core_ids=[0]).results[0]["out"]
```

```python
from contextlib import ExitStack

import concourse.bass as bass
from concourse import mybir

F32 = mybir.dt.float32
BF16 = mybir.dt.bfloat16
I32 = mybir.dt.int32
F16 = mybir.dt.float16
FP8 = mybir.dt.float8e4
ALU = mybir.AluOpType
ACT = mybir.ActivationFunctionType
AX = mybir.AxisListType.X

P = 128
N, E, D = 6250, 206250, 64
BN = 125
NB = N // BN
WN = 5
WB = BN // WN
WGRP = -(-NB * WB // P)
WT = 2
WE = WT * P
KW = NB * WN
BT = 34
BE = BT * P
TAIL = E - (E // P) * P
ROWS = 1650
EP = ROWS * P
SAMP = -(-E // P)
SCOLS = -(-SAMP // P)
TCOLS = WGRP + 1
FAR = 20000.0
MAGIC = 12582912.0
LN_EPS = 1e-5
MOST = 15.0
HW = 3 * D
XW = 2 * D + 1
XP = XW + 1
LOW = 4096.0
PITCH = P
RING = 5
OG = 5
LG = 7
OR = 5


NT = SAMP
DUP = 65536.0


class Count:

    def __init__(self, sem):
        self.sem, self.base, self.n = sem, 0, 0

    def __call__(self, ins, by=1):
        ins.then_inc(self.sem, by)
        self.n += by
        return self.base + self.n

    @property
    def now(self):
        return self.base + self.n

    def enter(self, i, per):
        self.start = self.now
        self.per = per
        self.base, self.n = self.start + i * per if per else self.start, 0

    def leave(self, trips):
        assert self.n == self.per, (self.n, self.per)
        self.base, self.n = self.start + trips * self.per, 0


def build(nc, x_t, cj_t, ci_t, src, dst, samples, edge_attr, ps_w, w1, b1, w2, b2, w3, w3o, b3s, b3i, b3o,
          w4a, b4a, w4b, b4b, eps, out):
    src_rows = src.rearrange("(r e) -> r e", e=P)
    dst_rows = dst.rearrange("(r e) -> r e", e=P)
    src_flat = src.rearrange("(a e) -> a e", a=1)
    dst_flat = dst.rearrange("(a e) -> a e", a=1)
    bst_dram = nc.dram_tensor("bst_dram", (NB + 2, 1), I32).ap()
    wst_dram = nc.dram_tensor("wst_dram", (WGRP * P + 1, 1), F32).ap()
    row_dram = nc.dram_tensor("row_dram", (N, D), F32).ap()
    sum_dram = nc.dram_tensor("sum_dram", (N, HW), F32).ap()
    y_dram = nc.dram_tensor("y_dram", (N, D), F32).ap()
    at_dram = nc.dram_tensor("at_dram", (NB, P, NB * PITCH // 2), BF16).ap()
    a_dram = nc.dram_tensor("a_dram", (NB, P, NB * PITCH // 2), BF16).ap()

    with ExitStack() as ctx:
        def sb(name, shape, dt, c=ctx):
            return c.enter_context(nc.sbuf_tensor(name, shape, dt))

        def sem(name):
            return ctx.enter_context(nc.semaphore(name))

        iota_key = sb("iota_key", [P, KW], BF16)
        iota_f = sb("iota_f", [P, BN + 3], F32)
        ident_f = sb("ident_f", [P, P], F32)
        ident_b = sb("ident_b", [P, P], BF16)
        thr_i = sb("thr_i", [P, TCOLS], I32)
        thr = sb("thr", [P, TCOLS], F32)
        cj = sb("cj", [BN, NB], F32)
        ci = sb("ci", [BN, NB], F32)
        psw = sb("psw", [P, D], F32)
        W1 = sb("W1", [P, D], F32)
        W2 = sb("W2", [P, D], F32)
        W3 = sb("W3", [P, D], F32)
        W3o = sb("W3o", [D, D], F32)
        W4a = sb("W4a", [D, 4 * D], F32)
        W4b = sb("W4b", [P, 2, D], F32)
        bias = sb("bias", [P, 6, D], F32)
        b4 = sb("b4", [P, 2], F32)
        ope = sb("ope", [P, 1], F32)
        epsc = sb("epsc", [P, 1], F32)
        most = sb("most", [P, 1], F32)
        lowt = sb("lowt", [BN, D], F32)
        ones_b = sb("ones_b", [P, 1], BF16)
        rowf = sb("rowf", [P, TCOLS], F32)
        rowi = sb("rowi", [P, TCOLS], I32)
        below = sb("below", [P, TCOLS], F32)
        starts = sb("starts", [P, TCOLS], I32)
        bstart = sb("bstart", [P, 1], I32)
        base = sb("base", [P, NB], F32)
        nxt = sb("nxt", [P, TCOLS], F32)
        total = sb("total", [P, 2], F32)
        slow = sb("slow", [1, 1], I32)
        overc = sb("overc", [P, 2, 5], F32)
        over = sb("over", [P, NB * 5 + 4], F32)
        XS = sb("XS", [BN, NB, D], F32)
        with ExitStack() as early:
            EW = sb("EW", [P, 3, WGRP * WE], F32, early)
        XN = sb("XN", [P, 2, NB, XP], F16)
        with ExitStack() as lay0:
            OHW = sb("OHW", [P, OR * LG, BN], F32, lay0)
        XH = sb("XH", [P, NB, HW], BF16)
        RC = sb("RC", [BN, NB], F32)
        KEYT = sb("KEYT", [P, WT, WGRP * P], F32)
        LOT = sb("LOT", [P, WT, WGRP * P], F32)
        keyc = sb("keyc", [P, 2, WT, WB], F32)
        loc = sb("loc", [P, 2, WT, WB], F32)
        srcc = sb("srcc", [P, 2, BT], I32)
        dstc = sb("dstc", [P, 2, BT], I32)
        dlc = sb("dlc", [P, 2, BT], F32)
        pac = sb("pac", [P, 2, BT], F32)
        lnst = sb("lnst", [BN, 6], F32)
        lnmv = sb("lnmv", [BN, RING, 2], F32)
        lnsd = sb("lnsd", [BN, RING], F32)
        lnrs = sb("lnrs", [BN, RING], F32)
        Z = sb("Z", [BN, RING, D], F32)
        R = sb("R", [BN, D], F32)
        with ExitStack() as pro:
            T1 = sb("T1", [P, WGRP, WE], F32, pro)
            T3 = sb("T3", [P, WGRP, WE], F32, pro)
            iota_i = sb("iota_i", [P, KW], I32, pro)
            base_i = sb("base_i", [P, NB], I32, pro)
            ytile = sb("ytile", [BN, NB, D], F32, pro)
            dord = sb("dord", [P, E // P + 1], I32, pro)
            dgt = sb("dgt", [P, E // P], F32, pro)
            dend = sb("dend", [1, TAIL], I32, pro)
            dendf = sb("dendf", [1, TAIL], F32, pro)
        pairs = sb("pairs", [P, RING, NB * PITCH // 2], BF16)
        slots = pairs[:, :, :].bitcast(FP8)
        with ExitStack() as lay0:
            KOH = sb("KOH", [P, OR * WT * OG, KW], BF16, lay0)
            LOH = sb("LOH", [P, OR * WT * OG, P], BF16, lay0)
            ea = sb("ea", [P, 2, BT, D], F32, lay0)
            G = sb("G", [P, 2, BT, D], F32, lay0)
        HS = sb("HS", [BN, NB, D], F32)
        RP = sb("RP", [BN, D], F32)
        g_far = sb("g_far", [P, 1], I32)
        g_near = sb("g_near", [P, 1], I32)
        g_row = sb("g_row", [P, P], I32)
        g_edge = sb("g_edge", [P, D], F32)
        g_farf = sb("g_farf", [P, 1], F32)
        g_nearf = sb("g_nearf", [P, 1], F32)
        g_rowf = sb("g_rowf", [P, P], F32)
        g_same = sb("g_same", [P, P], F32)
        g_before = sb("g_before", [P, P], F32)
        g_tmp = sb("g_tmp", [P, P], F32)
        g_c = sb("g_c", [P, 4], F32)
        g_idx = sb("g_idx", [P, 3], I32)
        g_got = sb("g_got", [P, D], F32)
        g_msg = sb("g_msg", [P, HW], F32)
        g_acc = sb("g_acc", [P, HW], F32)
        GA = sb("GA", [BN, RING, HW], F32)
        OUTS = sb("OUTS", [BN, NB, D], F32)
        MX = sb("MX", [BN, RING, 2 * D], F32)
        MO = sb("MO", [BN, RING, D], F32)
        AG = sb("AG", [BN, D + 2], F32)
        AL = sb("AL", [BN, RING, D], F32)
        AC = sb("AC", [BN, 2, RING], F32)
        TS = sb("TS", [P, 2, P], F32)
        H1 = sb("H1", [P, 2, BN], F32)
        PS = ctx.enter_context(nc.psum_tensor("PS", [P, 8, 512], F32))

        win_of = [EW[:, k, :].rearrange("p (g e) -> p g e", e=WE) for k in range(3)]
        WDF, WSF, T2 = win_of
        WD, WS = WDF.bitcast(I32), WSF.bitcast(I32)
        samp_i = T1[:, 0, 0:SCOLS].bitcast(I32)
        samp_f = T1[:, 1, 0:SCOLS]
        every_i = EW[:, 1, 0:TCOLS * P].bitcast(I32)
        every = EW[:, 2, 0:TCOLS * P]
        masks = [t[:, :, :, :].rearrange("p b t d -> p (b t d)").bitcast(BF16)[:, k * TCOLS * P:(k + 1) * TCOLS * P]
                 for t in (ea, G) for k in range(2 * BT * D * 2 // (TCOLS * P))]
        masks.append(T3[:, :, :].rearrange("p g e -> p (g e)").bitcast(BF16)[:, 0:TCOLS * P])
        low = EW[:, 0, 0:TCOLS * P].rearrange("p (g e) -> p g e", e=P)
        low_i = low.bitcast(I32)
        junk = slots[:, RING - 1, :]
        in_x, in_w, in_samp = sem("in_x"), sem("in_w"), sem("in_samp")
        iota_done = sem("iota_done")
        counted = sem("counted")
        dve_step = sem("dve_step")
        settled_waits = sem("settled_waits")
        y_stored, bst_stored = sem("y_stored"), sem("bst_stored")
        order_in, wst_stored, next_in = sem("order_in"), sem("wst_stored"), sem("next_in")
        total_ready = sem("total_ready")
        total_sum = sem("total_sum")
        slow_ready = sem("slow_ready")
        gz = {n: sem("gen_" + n) for n in ("start", "prep", "edge", "step", "index", "dot", "sig", "msg", "sum",
                                           "added", "next", "block_in", "mv", "sd", "x1", "mask")}
        gz_in, gz_rows, gz_kept = ([sem(f"gen_{n}{c}") for c in range(6)] for n in ("in", "rows", "kept"))
        low_in, win_in = sem("low_in"), sem("win_in")
        src_in = [sem("src_in0"), sem("src_in1")]
        ahead_in = sem("ahead_in")
        ed_in = [sem("ed_in0"), sem("ed_in1")]
        dot_ready = sem("dot_ready")
        sig_ready = sem("sig_ready")
        checked = sem("checked")
        over_kept = sem("over_kept")
        split_ready = sem("split_ready")
        pool_step = sem("pool_step")
        col_ready = sem("col_ready")
        col_out = sem("col_out")

        cols = sem("cols")
        oh_ready = sem("oh_ready")
        win_ready = sem("win_ready")
        win_out = sem("win_out")
        tr_ready = sem("tr_ready")
        tr_out = sem("tr_out")
        ow_ready = sem("ow_ready")
        ow_used = sem("ow_used")
        h0_taken = sem("h0_taken")
        at_stored = [sem("at_stored0"), sem("at_stored1")]
        a_stored = [sem("a_stored0"), sem("a_stored1")]
        rows_in = [sem("rows_in0"), sem("rows_in1")]
        mv_ready = sem("mv_ready")
        sd_ready = sem("sd_ready")
        x3_ready = sem("x3_ready")

        slot_in = [sem(f"slot_in{u}") for u in range(RING)]
        slot_used = [sem(f"slot_used{u}") for u in range(RING)]
        agg_taken = sem("agg_taken")
        row_ready = sem("row_ready")
        mt_ready = sem("mt_ready")
        ts_ready = sem("ts_ready")
        h1_ready = sem("h1_ready")
        h1_out = sem("h1_out")
        o_ready = sem("o_ready")
        o_taken = sem("o_taken")
        out_ready = sem("out_ready")
        out_stored = sem("out_stored")

        V = {}
        batches = [(a, h, list(range(g, min(g + 4, WGRP)))) for a in range(2) for h in range(WT)
                   for g in range(0, WGRP, 4)]
        NBAT = len(batches)
        GR, LR = WB // OG, -(-BT // LG)
        BANKS = ((0, 1), (2, 3), (4,))
        NBK = len(BANKS)
        WOUT = GR * NBK
        TB = 4
        TROUT = -(-NB // TB)
        CHK = LR
        TSPLIT = [TROUT * g // LR for g in range(LR + 1)]
        COLS = 2
        NG = NB // RING
        PREPS = [NG + 1] + [NG + 1] * 5
        F_OF = {0: 0, 1: 1, 3: 2, 4: 3}
        TS0 = {0: 0, 1: NB, 3: 2 * NB, 4: 4 * NB}
        NORM0 = {1: NB, 3: 2 * NB, 4: 3 * NB}
        X_IN = (XN[:, 0], XH, XN[:, 0], XN[:, 0], XN[:, 1])
        GROUP_STEPS = 6

        def group_sums(odd):
            flat = PS[:, 3 * odd:3 * odd + 3, :].rearrange("p b (h c) -> p (b h) c", h=2)
            return flat[:, 0:RING, 0:XW]

        X_NEED = (NB, 2 * NB, 3 * NB, 3 * NB, 4 * NB)

        def settled(e):
            e.sem_inc(settled_waits, 1)

        def need(e, s, v):
            if not isinstance(v, int) or v > 0:
                e.wait_ge(s, v)

        block = ctx.enter_context(nc.Block())

        @block.vector
        def _(e):
            st = Count(dve_step)

            def step(ins, wait=True):
                v = st(ins)
                if wait:
                    e.wait_ge(dve_step, v)
                return v

            def mark(c, ins, by=1):
                v = c(ins, by)
                e.wait_ge(c.sem, v)

            e.wait_ge(iota_done, 2)
            step(e.tensor_copy(iota_key[:, :], iota_i[:, :]), False)
            step(e.tensor_copy(iota_f[:, :], iota_i[:, 0:BN + 3]), False)
            step(e.tensor_copy(ident_b[:, :], ident_f[:, :]), False)
            step(e.tensor_copy(base[:, :], base_i[:, :]), False)
            step(e.memset(epsc[:, :], LN_EPS), False)
            step(e.memset(ones_b[:, :], 1.0), False)
            step(e.tensor_copy(every, every_i), False)
            step(e.memset(most[:, :], -MOST), False)
            step(e.tensor_copy(thr[:, :], thr_i[:, :]))
            e.wait_ge(in_samp, 16)
            step(e.tensor_copy(samp_f, samp_i))
            for c in range(SCOLS):
                step(e.tensor_scalar(masks[c], every, samp_f[:, c:c + 1], None, ALU.is_gt), False)
            V["masks"] = st.now
            e.wait_ge(counted, 1)
            step(e.tensor_scalar(rowf[:, :], PS[:, 0, 0:TCOLS], 1.0, 0.0, ALU.subtract, ALU.max))
            step(e.tensor_copy(rowi[:, :], rowf[:, :]))
            V["rows"] = st.now
            e.wait_ge(in_x, 48)
            step(e.tensor_tensor(ytile[:, :, :], XS[:, :, :], cj[:, :].unsqueeze(2).to_broadcast([BN, NB, D]), ALU.mult), False)
            V["y"] = st.now
            e.wait_ge(in_w, 16 * 15)
            step(e.tensor_scalar(W3[0:D, :], W3[0:D, :], 0.5, None, ALU.mult), False)
            step(e.tensor_scalar(W3o[:, :], W3o[:, :], 0.5, None, ALU.mult), False)
            step(e.tensor_scalar(ope[:, :], ope[:, :], 1.0, None, ALU.add), False)
            step(e.tensor_tensor(bias[:, 3, :], bias[:, 3, :], bias[:, 4, :], ALU.add))
            step(e.scalar_tensor_tensor(bias[:, 2, :], bias[:, 3, :], 0.5, bias[:, 2, :], ALU.mult, ALU.add))
            e.wait_ge(low_in, 16 * TCOLS)
            step(e.tensor_copy(low, low_i))
            step(e.tensor_tensor(low, low, thr[:, :].unsqueeze(2).to_broadcast([P, TCOLS, P]), ALU.is_lt))
            step(e.tensor_reduce(below[:, :], low, AX, ALU.add))
            step(e.scalar_tensor_tensor(below[:, :], rowf[:, :], float(P), below[:, :], ALU.mult, ALU.add))
            step(e.tensor_copy(starts[:, :], below[:, :]), False)
            step(e.tensor_scalar(bstart[:, :], below[:, WGRP:TCOLS], float(E - BE), None, ALU.min))
            V["starts"] = st.now
            e.wait_ge(order_in, 32)
            k = E // P
            step(e.memset(over[:, :], 0.0))
            step(e.tensor_tensor(dgt[:, :], dord[:, 0:k], dord[:, 1:k + 1], ALU.is_gt), False)
            step(e.tensor_tensor(dendf[:, 0:TAIL - 1], dend[:, 0:TAIL - 1], dend[:, 1:TAIL], ALU.is_gt))
            step(e.tensor_reduce(over[:, CHK * NB:CHK * NB + 1], dgt[:, :], AX, ALU.add), False)
            step(e.tensor_reduce(over[0:1, CHK * NB + 1:CHK * NB + 2], dendf[:, 0:TAIL - 1], AX, ALU.add), False)
            e.wait_ge(win_in, 16 * 2 * WGRP)
            step(e.tensor_copy(T1[:, :, :], WS))
            step(e.tensor_scalar(T2, T1[:, :, :], 1.0 / BN, 0.5 / BN - 0.5, ALU.mult, ALU.add))
            step(e.tensor_scalar(T2, T2, MAGIC, None, ALU.add))
            step(e.tensor_scalar(T2, T2, MAGIC, None, ALU.subtract))
            step(e.scalar_tensor_tensor(T1[:, :, :], T2, -float(BN), T1[:, :, :], ALU.mult, ALU.add), False)
            step(e.tensor_copy(T3[:, :, :], WD))
            step(e.tensor_tensor(T3[:, :, :], T3[:, :, :], thr[:, 0:WGRP].unsqueeze(2).to_broadcast([P, WGRP, WE]), ALU.subtract))
            step(e.tensor_scalar(WDF, T3[:, :, :], 0.0, FAR, ALU.is_lt, ALU.mult), False)
            step(e.tensor_scalar(WSF, T3[:, :, :], WN - 0.5, FAR, ALU.is_gt, ALU.mult))
            step(e.scalar_tensor_tensor(T3[:, :, :], T2, float(WN), T3[:, :, :], ALU.mult, ALU.add))
            step(e.tensor_tensor(T3[:, :, :], T3[:, :, :], WDF, ALU.add))
            step(e.tensor_tensor(T3[:, :, :], T3[:, :, :], WSF, ALU.add))
            V["keys"] = st.now
            e.wait_ge(next_in, 32)
            step(e.tensor_tensor(nxt[:, 0:WGRP], nxt[:, 0:WGRP], below[:, 0:WGRP], ALU.subtract), False)
            step(e.tensor_copy(total[0:NB, 0:1], bstart[0:NB, :]))
            step(e.tensor_tensor(nxt[0:NB, WGRP:TCOLS], nxt[0:NB, WGRP:TCOLS], total[0:NB, 0:1], ALU.subtract), False)
            step(e.tensor_scalar(nxt[:, 0:WGRP], nxt[:, 0:WGRP], float(WE), 0.0, ALU.subtract, ALU.max))
            step(e.tensor_scalar(over[0:NB, CHK * NB + 3:CHK * NB + 4], nxt[0:NB, WGRP:TCOLS], float(BE), 0.0, ALU.subtract, ALU.max), False)
            step(e.tensor_reduce(over[:, CHK * NB + 2:CHK * NB + 3], nxt[:, 0:WGRP], AX, ALU.add), False)
            step(e.memset(XN[:, 0, :, 0:XW - 1], 0.0), False)
            step(e.memset(XN[:, 0, :, XW - 1:XP], 1.0), False)
            e.wait_ge(y_stored, 16)
            e.wait_ge(col_ready, NBAT)
            pad = pairs[:, 0:2, :].rearrange("p b (h c) -> p (b h) c", c=PITCH // 2)[:, :, BN // 2:PITCH // 2]
            step(e.memset(pad, 0.0), False)
            step(e.memset(pairs[96:P, 2:4, :].bitcast(F32), 0.0))
            V["slots"] = st.now

            ohr, owr, taken = Count(oh_ready), Count(ow_ready), Count(h0_taken)
            mvr, x3r = Count(mv_ready), Count(x3_ready)
            aggt, ot, rowr, outr = Count(agg_taken), Count(o_taken), Count(row_ready), Count(out_ready)

            def at(t, j):
                return t[:, bass.ds(j, 1), :].rearrange("p a d -> p (a d)")

            def statistics(u=0):
                step(e.bn_stats(lnst[:, :], Z[:, u, :]))
                settled(e)
                mvr(e.bn_aggr(lnmv[:, u, :], lnst[:, :]))

            def normed(to, last=None):
                e.wait_ge(sd_ready, mvr.now)
                step(e.reciprocal(lnrs[:, 0:1], lnsd[:, 0:1]))
                ins = e.tensor_scalar(to, Z[:, 0, :], lnmv[:, 0, 0:1], lnrs[:, 0:1], ALU.subtract, ALU.mult)
                mark(last, ins) if last else step(ins)

            def split(v, j):
                row = XN[0:BN, 0, bass.ds(j, 1), :].rearrange("p a d -> p (a d)")
                step(e.tensor_copy(row[:, 0:D], v))
                step(e.tensor_tensor(R[:, :], v, row[:, 0:D], ALU.subtract))
                x3r(e.tensor_scalar(row[:, D:2 * D], R[:, :], LOW, None, ALU.mult))

            dotr, spl = Count(dot_ready), Count(split_ready)
            counts = (st, mvr, x3r, aggt, ot, rowr, outr, spl, taken, ohr, owr, dotr)

            def loop(trips, body, grow):
                with e.Fori(0, trips) as i:
                    for c, n in zip(counts, grow):
                        c.enter(i, n)
                    body(i)
                    for c in counts:
                        c.leave(trips)

            def rows_stats(j, b):
                e.wait_ge(ow_used, LR * (j + 1))
                mark(taken, e.scalar_tensor_tensor(Z[:, 0, :], PS[0:BN, 5 + b, 0:D], ci[:, bass.ds(j, 1)], at(XS, j),
                                                   ALU.mult, ALU.add))
                statistics()

            def rows_done(j):
                normed(at(XS, j))
                split(at(XS, j), j)

            def build_turn(i, first=False):
                for b in range(2):
                    j = 2 * i + b
                    e.wait_ge(ed_in[b], 32 * (i + 1))
                    need(e, ow_ready, LR * (j - 1))
                    step(e.tensor_scalar(dlc[:, b, :], dstc[:, b, :], base[:, bass.ds(j, 1)], None, ALU.subtract), False)
                    step(e.tensor_tensor(ea[:, b, :, :], ea[:, b, :, :], psw[:, :].unsqueeze(1).to_broadcast([P, BT, D]), ALU.mult))
                    dotr(e.tensor_reduce(pac[:, b, :], ea[:, b, :, :], AX, ALU.add))
                    e.wait_ge(cols, COLS * (j + 1))
                    for g in range(GR):
                        n = b * GR + g
                        need(e, win_ready, NBK * (2 * GR * i + n - OR + 1))
                        for w in range(OG):
                            for h in range(WT):
                                t = (n % OR * OG + w) * WT + h
                                W = g * OG + w
                                e.tensor_scalar(KOH[:, t, :], iota_key[:, :], keyc[:, b, h, W:W + 1], None, ALU.is_equal)
                                ins = e.tensor_scalar(LOH[:, t, :], iota_key[:, 0:P], loc[:, b, h, W:W + 1], None, ALU.is_equal)
                        ohr(ins)
                        if g == 1 and not first:
                            rows_done(j - 2)
                    e.wait_ge(sig_ready, j + 1)
                    for g in range(LR):
                        n = b * LR + g
                        need(e, ow_used, 2 * LR * i + n - OR + 1)
                        for q in range(min(LG, BT - g * LG)):
                            t = g * LG + q
                            ins = e.tensor_scalar(OHW[:, (n % OR) * LG + q, :], iota_f[:, 0:BN], dlc[:, b, t:t + 1],
                                                  pac[:, b, t:t + 1], ALU.is_equal, ALU.mult)
                        owr(ins)
                        if g == 1 and not (first and b == 0):
                            rows_stats(j - 1, 1 - b)

            build_turn.grow = (2 * 7, 2, 2, 0, 0, 0, 0, 0, 2, 2 * GR, 2 * LR, 2)
            build_turn(0, True)
            loop(NB // 2 - 1, lambda i: build_turn(i + 1), build_turn.grow)
            rows_done(NB - 2)
            rows_stats(NB - 1, 1)
            rows_done(NB - 1)
            e.wait_ge(ed_in[0], 32 * (NB // 2 + 1))
            e.wait_ge(src_in[0], 16 * (NB // 2 + 1))

            e.wait_ge(over_kept, NB)
            step(e.memset(total[:, 1:2], 1.0))
            step(e.tensor_reduce(total[:, 0:1], over[:, :], AX, ALU.add))
            e.tensor_scalar(total[:, 0:1], total[:, 0:1], float(E), None, ALU.min).then_inc(total_ready, 1)
            e.wait_ge(total_sum, 1)
            e.tensor_scalar(slow[:, :], PS[0:1, 7, 0:1], 0.0, 0.0, ALU.is_le, ALU.is_equal).then_inc(slow_ready, 1)
            step(e.memset(XH[:, :, :].bitcast(F32), 0.0))
            step(e.memset(XN[:, 1, :, :], 0.0))
            e.wait_ge(slow_ready, 1)
            general = e.value_load(slow[0:1, 0:1], min_val=0, max_val=1)

            gs = Count(gz["step"])

            def gstep(ins):
                e.wait_ge(gz["step"], gs(ins))
                settled(e)

            def general_sums(c, swap, count):
                gstep(e.memset(g_msg[:, :], 0.0))
                gstep(e.memset(GA[:, :, :], 0.0))
                e.sem_inc(gz["start"], 1)
                with e.Fori(0, NT) as t:
                    gs.enter(t, 12 if c == 0 else 10)
                    n = NT * c + t + 1
                    e.wait_ge(gz_in[c], 48 * (t + 1))
                    if c == 0:
                        e.wait_ge(gz["edge"], 16 * (t + 1))
                    settled(e)
                    gstep(e.tensor_copy(g_farf[:, :], g_far[:, :]))
                    gstep(e.tensor_copy(g_nearf[:, :], g_near[:, :]))
                    gstep(e.tensor_copy(g_rowf[:, :], g_row[:, :]))
                    gstep(e.tensor_scalar(g_c[:, 0:1], (g_farf if swap else g_nearf)[:, :], N - 0.5, None, ALU.is_lt))
                    gstep(e.tensor_scalar(g_idx[:, 0:1], g_farf[:, :], N - 1.0, None, ALU.min))
                    gstep(e.tensor_scalar(g_idx[:, 1:2], g_nearf[:, :], N - 1.0, None, ALU.min))
                    gstep(e.tensor_scalar(g_same[:, :], g_rowf[:, :], g_nearf[:, 0:1], None, ALU.is_equal))
                    gstep(e.tensor_tensor(g_tmp[:, :], g_same[:, :], g_before[:, :], ALU.mult))
                    gstep(e.tensor_reduce(g_c[:, 1:2], g_tmp[:, :], AX, ALU.add))
                    e.scalar_tensor_tensor(g_idx[:, 2:3], g_c[:, 1:2], DUP, g_nearf[:, :], ALU.mult, ALU.add).then_inc(gz["index"], 1)
                    if c == 0:
                        gstep(e.tensor_tensor(g_edge[:, :], g_edge[:, :], psw[:, :], ALU.mult))
                        e.tensor_reduce(g_c[:, 2:3], g_edge[:, :], AX, ALU.add).then_inc(gz["dot"], 1)
                        e.wait_ge(gz["sig"], t + 1)
                        settled(e)
                        gstep(e.tensor_tensor(g_c[:, 3:4], g_c[:, 2:3], g_c[:, 0:1], ALU.mult))
                    weight = g_c[:, 3:4] if c == 0 else g_c[:, 0:1]
                    if count:
                        gstep(e.tensor_copy(g_msg[:, 2 * D:2 * D + 1], g_c[:, 0:1]))
                    else:
                        gstep(e.memset(g_msg[:, 2 * D:2 * D + 1], 0.0))
                    e.wait_ge(gz_rows[c], 32 * (t + 1))
                    settled(e)
                    e.tensor_scalar(g_msg[:, 0:D], g_got[:, :], weight, None, ALU.mult).then_inc(gz["msg"], 1)
                    e.wait_ge(gz["sum"], n)
                    settled(e)
                    e.tensor_tensor(g_acc[:, :], g_acc[:, :], PS[:, 6, 0:HW], ALU.add).then_inc(gz["added"], 1)
                    e.wait_ge(gz["added"], n)
                    gs.leave(NT)

            with e.If(general > 0):
                general_sums(0, False, False)
                with e.Fori(0, NB) as j:
                    gs.enter(j, 4)
                    e.wait_ge(gz["block_in"], 16 * (j + 1))
                    settled(e)
                    gstep(e.scalar_tensor_tensor(Z[:, 0, :], GA[:, 0, 0:D], ci[:, bass.ds(j, 1)], at(XS, j), ALU.mult, ALU.add))
                    gstep(e.bn_stats(lnst[:, :], Z[:, 0, :]))
                    settled(e)
                    e.bn_aggr(lnmv[:, 0, :], lnst[:, :]).then_inc(gz["mv"], 1)
                    e.wait_ge(gz["sd"], j + 1)
                    settled(e)
                    gstep(e.reciprocal(lnrs[:, 0:1], lnsd[:, 0:1]))
                    gstep(e.tensor_scalar(at(XS, j), Z[:, 0, :], lnmv[:, 0, 0:1], lnrs[:, 0:1], ALU.subtract, ALU.mult))
                    e.sem_inc(gz["x1"], 1)
                    gs.leave(NB)

            def gather_in(p, j, u):
                inv = RC[:, bass.ds(j, 1)]
                if p == 0:
                    step(e.tensor_scalar(AG[:, D:D + 1], PS[0:BN, u, 2 * D:XW], 1.0, None, ALU.max))
                    step(e.reciprocal(inv, AG[:, D:D + 1]))
                high = PS[0:BN, u, 0:D]
                if p == 1:
                    step(e.tensor_copy(MX[:, u, D:2 * D], at(HS, j)), False)
                    mark(aggt, e.tensor_reduce(AG[:, 0:D], PS[0:BN, u, 0:HW].rearrange("p (q d) -> p d q", d=D), AX, ALU.add))
                    mark(rowr, e.tensor_scalar(MX[:, u, 0:D], AG[:, 0:D], inv, None, ALU.mult))
                    return
                if p == 4:
                    step(e.scalar_tensor_tensor(AG[:, 0:D], at(XS, j), ope[0:BN, 0:1], high, ALU.mult, ALU.add))
                    mark(aggt, e.scalar_tensor_tensor(MX[:, u, 0:D], PS[0:BN, u, D:2 * D], 1.0 / LOW, AG[:, 0:D], ALU.mult, ALU.add))
                    return
                step(e.tensor_scalar(AG[:, 0:D], PS[0:BN, u, D:2 * D], inv, 1.0 / LOW, ALU.mult, ALU.mult))
                if p == 0:
                    step(e.tensor_copy(MX[:, u, D:2 * D], at(XS, j)), False)
                    to = MX[:, u, 0:D]
                else:
                    to = at(HS, j)
                mark(aggt, e.scalar_tensor_tensor(to, high, inv, AG[:, 0:D], ALU.mult, ALU.add))

            def group_in(p, g, odd):
                group = bass.ds(RING * g, RING)
                S = group_sums(odd)[0:BN, :, :]
                step(e.tensor_copy(MX[:, :, 0:D], HS[:, group, :]), False)
                step(e.tensor_copy(MX[:, :, D:2 * D], XS[:, group, :]), False)
                e.wait_ge(slot_used[RING - 1], NG * p + g + 1)
                settled(e)
                step(e.tensor_scalar(AC[:, 0, :], S[:, :, 2 * D], 1.0, None, ALU.max))
                step(e.reciprocal(AC[:, 1, :], AC[:, 0, :]))
                inv = AC[:, 1, :].unsqueeze(2).to_broadcast([BN, RING, D])
                step(e.tensor_tensor(AL[:, :, :], S[:, :, D:2 * D], inv, ALU.mult), False)
                step(e.tensor_tensor(MO[:, :, :], S[:, :, 0:D], inv, ALU.mult))
                mark(aggt, e.scalar_tensor_tensor(MO[:, :, :], AL[:, :, :], 1.0 / LOW, MO[:, :, :], ALU.mult, ALU.add), RING)

            def finish(p, j, u, prev):
                n = {0: 0, 1: 1, 3: 2, 4: 5}[p]
                if prev and p != 0:
                    up = (u - 1) % RING
                    e.wait_ge(sd_ready, mvr.now)
                    v = step(e.reciprocal(lnrs[:, up:up + 1], lnsd[:, up:up + 1]), False)
                e.wait_ge(o_ready, NB * F_OF[p] + j + 1)
                mark(ot, e.tensor_tensor(Z[:, u, :], PS[0:BN, 7, 0:D], bias[0:BN, n, :], ALU.add))
                if p == 0:
                    mark(spl, e.tensor_scalar(at(HS, j), Z[:, u, :], 0.0, None, ALU.max))
                    return
                if prev:
                    e.wait_ge(dve_step, v)
                    normalise(p, j - 1, up)
                step(e.tensor_tensor(Z[:, u, :], Z[:, u, :], at(XS, j), ALU.add))
                statistics(u)

            def normalise(p, j, u):
                (outr if p == 4 else spl)(e.tensor_scalar(at(XS if p < 4 else OUTS, j), Z[:, u, :], lnmv[:, u, 0:1], lnrs[:, u:u + 1],
                                                          ALU.subtract, ALU.mult))

            GROW = {0: (4, 0, 0, 1, 1, 0, 0, 1), 1: (1 + 3, 1, 0, 1, 1, 1, 0, 1), 2: (1, 0, 0, 1, 0, 0, 0, 0),
                    3: (3, 1, 0, 1, 1, 0, 0, 1), 4: (1 + 3, 1, 0, 1, 1, 0, 1, 0)}
            for p in range(5):
                def turn(g, gather, fin, odd=0, p=p, first=False):
                    for u in range(RING):
                        if gather and p != 3:
                            e.wait_ge(slot_used[u], NG * p + g + 1)
                            gather_in(p, RING * g + u, u)
                        if fin:
                            finish(p, RING * (g - 1) + u, u, not (first and u == 0))
                    if gather and p == 3:
                        group_in(p, g, odd)

                with e.If(general > 0):
                    general_sums(p + 1, p == 3, p in (0, 3))
                turn(0, True, False)
                turn(1, True, p != 2, 1, first=True)
                grow = tuple(RING * n for n in GROW[p]) + (0,) * 4
                if p == 3:
                    grow = tuple(2 * n for n in (grow[0] + GROUP_STEPS,) + grow[1:])

                    def both(i):
                        turn(2 * i + 2, True, True, 0)
                        turn(2 * i + 3, True, True, 1)

                    loop(NG // 2 - 1, both, grow)
                else:
                    loop(NG - 2, lambda i: turn(i + 2, True, p != 2), grow)
                if p != 2:
                    turn(NG, False, True)
                if p in (1, 3, 4):
                    e.wait_ge(sd_ready, mvr.now)
                    step(e.reciprocal(lnrs[:, RING - 1:RING], lnsd[:, RING - 1:RING]))
                    normalise(p, NB - 1, RING - 1)

        @block.gpsimd
        def _(e):
            e.iota(iota_i[:, :], pattern=[[1, KW]], base=0, channel_multiplier=0)
            e.iota(every_i[:, 0:WGRP * P], pattern=[[WN, WGRP * P]], base=0, channel_multiplier=0)
            e.iota(every_i[:, WGRP * P:TCOLS * P], pattern=[[BN, P]], base=0, channel_multiplier=0)
            e.iota(base_i[:, :], pattern=[[BN, NB]], base=0, channel_multiplier=0)
            e.iota(thr_i[:, 0:WGRP], pattern=[[WN * P, WGRP]], base=0, channel_multiplier=WN)
            e.iota(thr_i[:, WGRP:TCOLS], pattern=[[0, 1]], base=0, channel_multiplier=BN)
            e.memset(lowt[:, :], LOW)
            e.memset(ident_f[:, :], 0.0).then_inc(iota_done, 1)
            e.wait_ge(iota_done, 1)
            e.affine_select(out=ident_f[:, :], in_=ident_f[:, :], compare_op=ALU.not_equal, fill=1.0,
                            base=0, pattern=[[-1, P]], channel_multiplier=1).then_inc(iota_done, 1)

            def gather(to, table, index, axis, s):
                e.indirect_dma_start(out=to, out_offset=None, in_=table,
                                     in_offset=bass.IndirectOffsetOnAxis(ap=index, axis=axis)).then_inc(s, 16)

            e.wait_ge(dve_step, V["rows"])
            for g in range(TCOLS):
                gather(low_i[:, g, :], dst_rows, rowi[:, g:g + 1], 0, low_in)
            e.wait_ge(dve_step, V["starts"])
            for g in range(WGRP):
                gather(WD[:, g, :], dst_flat, starts[:, g:g + 1], 1, win_in)
                gather(WS[:, g, :], src_flat, starts[:, g:g + 1], 1, win_in)
            e.wait_ge(y_stored, 16)

            def rows_turn(i):
                for b in range(2):
                    e.wait_ge(src_in[b], 16 * (i + 1))
                    need(e, ow_used, LR * (2 * i + b - 1))
                    settled(e)
                    for t in range(BT):
                        gather(G[:, b, t, :], y_dram, srcc[:, b, t:t + 1], 0, rows_in[b])

            rows_turn(0)
            with e.Fori(0, NB // 2 - 1) as i:
                rows_turn(i + 1)

            e.wait_ge(slow_ready, 1)
            general = e.value_load(slow[0:1, 0:1], min_val=0, max_val=1)

            def general_sums(c):
                e.wait_ge(gz["start"], c + 1)
                e.wait_ge(gz["prep"], 16 * sum(PREPS[:c + 1]))
                e.sem_inc(gz["next"], 1)
                table = y_dram if c == 0 else row_dram
                with e.Fori(0, NT) as t:
                    n = NT * c + t + 1
                    e.wait_ge(gz["index"], n)
                    settled(e)
                    gather(g_got[:, :], table, g_idx[:, 0:1], 0, gz_rows[c])
                    gather(g_acc[:, :], sum_dram, g_idx[:, 1:2], 0, gz_rows[c])
                    e.wait_ge(gz["added"], n)
                    settled(e)
                    e.indirect_dma_start(out=sum_dram, out_offset=bass.IndirectOffsetOnAxis(ap=g_idx[:, 2:3], axis=0),
                                         in_=g_acc[:, :], in_offset=None, bounds_check=N - 1, oob_is_err=False).then_inc(gz_kept[c], 16)
                    e.wait_ge(gz_kept[c], 16 * (t + 1))
                    e.sem_inc(gz["next"], 1)

            with e.If(general > 0):
                e.memset(g_before[:, :], 1.0).then_inc(gz["mask"], 1)
                e.wait_ge(gz["mask"], 1)
                e.affine_select(out=g_before[:, :], in_=g_before[:, :], compare_op=ALU.is_gt, fill=0.0,
                                base=0, pattern=[[-1, P]], channel_multiplier=1).then_inc(gz["mask"], 1)
                e.wait_ge(gz["mask"], 2)
                general_sums(0)
            st, x3r = Count(pool_step), Count(x3_ready)
            for f, p in enumerate((0, 1, 3)):
                with e.If(general > 0):
                    if p == 3:
                        general_sums(3)
                    general_sums(p + 1)
                with e.Fori(0, NB) as j:
                    st.enter(j, 3 if p == 0 else 2)
                    e.wait_ge(split_ready, NB * f + j + 1)
                    settled(e)
                    here = bass.ds(j, 1)
                    v = (HS if p == 0 else XS)[:, here, :].rearrange("p a d -> p (a d)")
                    to = (XH[0:BN, here, :] if p == 0 else XN[0:BN, 0 if p == 1 else 1, here, :]).rearrange("p a d -> p (a d)")

                    def step(ins):
                        e.wait_ge(pool_step, st(ins))
                        settled(e)

                    step(e.tensor_copy(to[:, 0:D], v))
                    step(e.tensor_tensor(RP[:, :], v, to[:, 0:D], ALU.subtract))
                    if p == 0:
                        step(e.tensor_copy(to[:, D:2 * D], RP[:, :]))
                        x3r(e.tensor_tensor(to[:, 2 * D:HW], RP[:, :], to[:, D:2 * D], ALU.subtract))
                    else:
                        x3r(e.tensor_tensor(to[:, D:2 * D], RP[:, :], lowt[:, :], ALU.mult))
                    e.wait_ge(x3_ready, NB * (f + 1) + j + 1)
                    st.leave(NB)
            with e.If(general > 0):
                general_sums(5)
            outv = out.rearrange("(b p) d -> p b d", p=BN)
            with e.Fori(0, NG) as g:
                e.wait_ge(out_ready, RING * (g + 1))
                e.dma_start(outv[:, bass.ds(RING * g, RING), :], OUTS[:, bass.ds(RING * g, RING), :]).then_inc(out_stored, 16)
            e.wait_ge(out_stored, 16 * NG)

        @block.sync
        def _(e):
            e.dma_start(samp_i, samples).then_inc(in_samp, 16)
            e.dma_start(XS[:, :, :], x_t).then_inc(in_x, 16)
            e.dma_start(cj[:, :], cj_t).then_inc(in_x, 16)
            e.dma_start(ci[:, :], ci_t).then_inc(in_x, 16)
            e.dma_start(psw[:, :], ps_w.to_broadcast([P, D])).then_inc(in_w, 16)
            with nc.allow_non_contiguous_dma(reason="a bias as a column"):
                for to, frm in ((W1[:, :], w1), (W2[:, :], w2), (W3[:, :], w3), (W3o[:, :], w3o), (W4a[:, :], w4a),
                                (W4b[:, :, :], w4b.rearrange("(c k) n -> k c n", c=2)),
                                (b4[:, :], b4a.rearrange("(c k) -> k c", c=2))):
                    e.dma_start(to, frm).then_inc(in_w, 16)
            for n, v in enumerate((b1, b2, b3s, b3i, b3o, b4b)):
                e.dma_start(bias[:, n, :], v.rearrange("(a d) -> a d", a=1).to_broadcast([P, D])).then_inc(in_w, 16)
            e.dma_start(ope[:, :], eps.rearrange("(a d) -> a d", a=1).to_broadcast([P, 1])).then_inc(in_w, 16)
            k = E // P
            ordered = bass.AP(tensor=dst.tensor, offset=0, ap=[[k, P], [1, k + 1]])
            e.dma_start(dord[:, :], ordered).then_inc(order_in, 16)
            e.dma_start(dend[:, :], dst[k * P:E].rearrange("(a n) -> a n", a=1)).then_inc(order_in, 16)
            e.wait_ge(dve_step, V["y"])
            e.dma_start(y_dram.rearrange("(b p) d -> p b d", p=BN), ytile[:, :, :]).then_inc(y_stored, 16)
            e.wait_ge(dve_step, V["starts"])
            e.dma_start(bst_dram, bstart[0:NB + 2, :]).then_inc(bst_stored, 16)
            e.wait_ge(bst_stored, 16)

            def load_edges(i, b):
                j = 2 * i + b
                need(e, rows_in[b], 16 * BT * i)
                settled(e)
                first = e.value_load(bst_dram[bass.ds(j, 1), :], min_val=0, max_val=E - BE)
                e.dma_start(srcc[:, b, :], src[bass.ds(first, BE)].rearrange("(p t) -> p t", t=BT)).then_inc(src_in[b], 16)
                need(e, ow_used, LR * (j - 1))
                e.dma_start(dstc[:, b, :], dst[bass.ds(first, BE)].rearrange("(p t) -> p t", t=BT)).then_inc(ed_in[b], 16)
                e.dma_start(ea[:, b, :, :], edge_attr[bass.ds(first, BE), :].rearrange("(p t) d -> p t d", t=BT)).then_inc(ed_in[b], 16)

            def store_turn(i):
                for b in range(2):
                    j = 2 * i + b
                    load_edges(i + b, 1 - b)
                    e.wait_ge(win_out, WOUT * (j + 1))
                    e.dma_start(at_dram[bass.ds(j, 1), :, :].rearrange("a p n -> (a p) n"), pairs[:, b, :]).then_inc(at_stored[b], 16)
                    e.wait_ge(tr_out, TROUT * (j + 1))
                    e.dma_start(a_dram[bass.ds(j, 1), :, :].rearrange("a p n -> (a p) n"), pairs[:, 2 + b, :]).then_inc(a_stored[b], 16)

            load_edges(0, 0)
            with nc.allow_non_contiguous_dma(reason="starts in the order of the windows"):
                e.dma_start(wst_dram[0:WGRP * P, :].rearrange("(g p) a -> p (g a)", p=P), below[:, 0:WGRP]).then_inc(wst_stored, 16)
                e.dma_start(wst_dram[WGRP * P:WGRP * P + 1, :], below[P - 1:P, WGRP - 1:WGRP]).then_inc(wst_stored, 16)
                e.wait_ge(wst_stored, 32)
                e.dma_start(nxt[:, 0:WGRP], wst_dram[1:WGRP * P + 1, :].rearrange("(g p) a -> p (g a)", p=P)).then_inc(next_in, 16)
                e.dma_start(nxt[0:NB, WGRP:TCOLS], wst_dram[WB:WB * (NB + 1), :].rearrange("(p w) a -> p (w a)", w=WB)[:, 0:1]).then_inc(next_in, 16)
            store_turn(0)
            with e.Fori(0, NB // 2 - 1) as i:
                store_turn(i + 1)
            for s in (*at_stored, *a_stored):
                e.wait_ge(s, 16 * (NB // 2))
            e.wait_ge(checked, CHK * NB)

            def load_turn(p, g):
                for u in range(RING):
                    need(e, slot_used[u], g + NG * p)
                    if p == 3:
                        rows = NB // RING
                        w = RING * PITCH // 2
                        to = pairs[:, u, :].rearrange("p (j n) -> p j n", n=w)
                        frm = a_dram[rows * u:rows * (u + 1), :, bass.ds(g * w, w)].rearrange("j p n -> p j n")
                    else:
                        to = pairs[:, u, :]
                        frm = at_dram[bass.ds(RING * g + u, 1), :, :].rearrange("a p n -> (a p) n")
                    e.dma_start(to, frm).then_inc(slot_in[u], 16)

            def general_sums(c, near, far):
                e.wait_ge(gz["start"], c + 1)
                for k in range(NG):
                    e.dma_start(sum_dram[k * RING * BN:(k + 1) * RING * BN, :].rearrange("(b p) d -> p b d", p=BN), GA[:, :, :]).then_inc(gz["prep"], 16)
                if c > 0:
                    rows = HS if c == 2 else XS
                    e.dma_start(row_dram.rearrange("(b p) d -> p b d", p=BN), rows[:, :, :]).then_inc(gz["prep"], 16)
                e.wait_ge(gz["prep"], 16 * sum(PREPS[:c + 1]))
                def edges(t, rows):
                    e.wait_ge(gz["next"], (NT + 1) * c + t + 1)
                    at = bass.ds(t * P, P)
                    e.dma_start(g_far[:, :], far[at].rearrange("(p a) -> p a", a=1)).then_inc(gz_in[c], 16)
                    e.dma_start(g_near[:, :], near[at].rearrange("(p a) -> p a", a=1)).then_inc(gz_in[c], 16)
                    e.dma_start(g_row[:, :], near[at].rearrange("(a p) -> a p", a=1).to_broadcast([P, P])).then_inc(gz_in[c], 16)
                    if c == 0:
                        e.dma_start(g_edge[0:rows, :], edge_attr[bass.ds(t * P, rows), :]).then_inc(gz["edge"], 16)

                with e.Fori(0, NT - 1) as t:
                    edges(t, P)
                edges(NT - 1, E - (NT - 1) * P)
                e.wait_ge(gz["next"], (NT + 1) * (c + 1))

            for u in range(RING):
                e.dma_start(pairs[:, u, :], at_dram[u, :, :]).then_inc(ahead_in, 16)
            e.wait_ge(slow_ready, 1)
            general = e.value_load(slow[0:1, 0:1], min_val=0, max_val=1)
            with e.If(general > 0):
                e.dma_start(XS[:, :, :], x_t).then_inc(gz["prep"], 16)
                general_sums(0, dst, src)
                e.dma_start(GA[:, 0, :], sum_dram[0:BN, :]).then_inc(gz["block_in"], 16)
                with e.Fori(1, NB) as j:
                    e.wait_ge(gz["x1"], j)
                    e.dma_start(GA[:, 0, :], sum_dram[bass.ds(j * BN, BN), :]).then_inc(gz["block_in"], 16)
                e.wait_ge(gz["x1"], NB)
            for p in range(5):
                with e.If(general > 0):
                    if p > 0:
                        e.wait_ge(x3_ready, X_NEED[p])
                    general_sums(p + 1, *((src, dst) if p == 3 else (dst, src)))

                    def sums_turn(g):
                        for u in range(RING):
                            need(e, slot_used[u], g + NG * p)
                            e.dma_start(GA[:, u, :], sum_dram[bass.ds((RING * g + u) * BN, BN), :]).then_inc(slot_in[u], 16)

                    sums_turn(0)
                    with e.Fori(1, NG) as g:
                        sums_turn(g)
                with e.Else():
                    if p == 0:
                        e.wait_ge(ahead_in, 16 * RING)
                        for u in range(RING):
                            e.sem_inc(slot_in[u], 16)
                    else:
                        load_turn(p, 0)
                    with e.Fori(0, NG - 1) as g:
                        load_turn(p, g + 1)

        @block.scalar
        def _(e):
            for n, (a, h, items) in enumerate(batches):
                e.wait_ge(col_ready, n + 1)
                to = (KEYT, LOT)[a][:, h, items[0] * P:(items[-1] + 1) * P]
                e.activation(to, PS[:, n % 2, 0:len(items) * P], ACT.Copy).then_inc(col_out, 1)
            e.wait_ge(col_out, NBAT)
            e.wait_ge(dve_step, V["slots"])

            def windows(j, b):
                need(e, oh_ready, GR * (j - 1))
                window = bass.ds(j * WB, WB)
                e.activation(keyc[:, b, :, :], KEYT[:, :, window], ACT.Copy).then_inc(cols, 1)
                e.activation(loc[:, b, :, :], LOT[:, :, window], ACT.Copy).then_inc(cols, 1)

            def deviation(j):
                e.wait_ge(mv_ready, j + 1)
                e.activation(lnsd[:, 0:1], lnmv[:, 0, 1:2], ACT.Sqrt, bias=epsc[0:BN, 0:1]).then_inc(sd_ready, 1)

            def build_turn(i, first=False):
                for b in range(2):
                    j = 2 * i + b
                    windows(j + 1, 1 - b)
                    e.wait_ge(dot_ready, j + 1)
                    e.activation(pac[:, b, :], pac[:, b, :], ACT.Sigmoid).then_inc(sig_ready, 1)
                    need(e, at_stored[b], 16 * i)
                    need(e, over_kept, j - 1)
                    slot = slots[:, b, :].rearrange("p (h c) -> p h c", c=PITCH)[:, :, 0:BN].rearrange("p h (w l) -> p w h l", l=WN)
                    for g in range(GR):
                        for k, ws in enumerate(BANKS):
                            e.wait_ge(win_ready, WOUT * j + NBK * g + k + 1)
                            w = OG * g + ws[0]
                            settled(e)
                            e.activation(slot[:, w:w + len(ws), :, :],
                                         PS[:, k, 0:len(ws) * KW].rearrange("p (w h l) -> p w h l", h=NB, l=WN),
                                         ACT.Copy, saturate=False).then_inc(win_out, 1)
                    need(e, a_stored[b], 16 * i)
                    slot = slots[0:BN, 2 + b, :].rearrange("p (h c) -> p h c", c=PITCH)
                    for n in range(TROUT):
                        h0, h1 = TB * n, min(TB * n + TB, NB)
                        e.wait_ge(tr_ready, TROUT * j + n + 1)
                        bank = PS[0:BN, 3 + (b * TROUT + n) % 2, :].rearrange("p (h c) -> p h c", c=PITCH)
                        settled(e)
                        e.activation(slot[:, h0:h1, :], bank[:, 0:h1 - h0, :], ACT.Copy, saturate=False).then_inc(tr_out, 1)
                        if n == TSPLIT[2] - 1 and not (first and b == 0):
                            deviation(j - 1)
                        if n + 1 in TSPLIT:
                            k = TSPLIT.index(n + 1) - 1
                            cw = NB * PITCH // CHK
                            need(e, checked, CHK * (j - 1) + k + 1)
                            settled(e)
                            e.activation(junk[:, k * cw:(k + 1) * cw], slots[:, b, k * cw:(k + 1) * cw], ACT.Relu, bias=most[:, 0:1],
                                         saturate=False, accum_out=overc[:, b, k:k + 1]).then_inc(checked, 1)
                    e.wait_ge(checked, CHK * (j + 1))
                    e.activation(over[:, bass.ds(j * CHK, CHK)], overc[:, b, :], ACT.Copy).then_inc(over_kept, 1)

            windows(0, 0)
            build_turn(0, True)
            with e.Fori(0, NB // 2 - 1) as i:
                build_turn(i + 1)
            deviation(NB - 1)
            e.wait_ge(slow_ready, 1)
            general = e.value_load(slow[0:1, 0:1], min_val=0, max_val=1)
            with e.If(general > 0):
                with e.Fori(0, NT) as t:
                    e.wait_ge(gz["dot"], t + 1)
                    e.activation(g_c[:, 2:3], g_c[:, 2:3], ACT.Sigmoid).then_inc(gz["sig"], 1)
                with e.Fori(0, NB) as j:
                    e.wait_ge(gz["mv"], j + 1)
                    e.activation(lnsd[:, 0:1], lnmv[:, 0, 1:2], ACT.Sqrt, bias=epsc[0:BN, 0:1]).then_inc(gz["sd"], 1)
            for p in (0, 1, 3, 4):
                def spread(j, u, p=p):
                    e.wait_ge(mv_ready, NORM0[p] + j + 1)
                    e.activation(lnsd[:, u:u + 1], lnmv[:, u, 1:2], ACT.Sqrt, bias=epsc[0:BN, 0:1]).then_inc(sd_ready, 1)

                def out_turn(g, first, p=p, spread=spread):
                    for u in range(RING):
                        j = RING * g + u
                        e.wait_ge(mt_ready, NB * F_OF[p] + j + 1)
                        k = D if p == 4 else P
                        e.activation(TS[0:k, 0, 0:BN], PS[0:k, 6 if p == 3 else 5, 0:BN], ACT.Copy).then_inc(ts_ready, 1)
                        if p == 3:
                            e.activation(TS[0:D, 1, 0:BN], PS[0:D, 6, P:P + BN], ACT.Copy).then_inc(ts_ready, 1)
                        if p == 4:
                            e.wait_ge(h1_ready, j + 1)
                            for c in range(2):
                                e.activation(H1[:, c, :], PS[:, 6, c * P:c * P + BN], ACT.Identity, bias=b4[:, c:c + 1]).then_inc(h1_out, 1)
                        if p != 0 and not (first and u == 0):
                            spread(j - 1, (u - 1) % RING)

                out_turn(0, True)
                with e.Fori(1, NG) as g:
                    out_turn(g, False)
                if p != 0:
                    spread(NB - 1, RING - 1)

        @block.tensor
        def _(e):
            e.wait_ge(dve_step, V["masks"])
            for g in range(TCOLS):
                for c in range(SCOLS):
                    ins = e.matmul(PS[:, 0, g:g + 1], masks[c][:, g * P:(g + 1) * P], ones_b[:, :], start=c == 0, stop=c == SCOLS - 1)
            ins.then_inc(counted, 1)
            e.wait_ge(dve_step, V["keys"])
            for n, (a, h, items) in enumerate(batches):
                if n >= 2:
                    e.wait_ge(col_out, n - 1)
                for k, it in enumerate(items):
                    frm = (T3, T1)[a][:, it, h * P:(h + 1) * P]
                    ins = e.transpose(PS[:, n % 2, k * P:(k + 1) * P], frm, ident_f[:, :])
                ins.then_inc(col_ready, 1)
            e.wait_ge(col_out, NBAT)

            def build_turn(i):
                for b in range(2):
                    j = 2 * i + b
                    for g in range(GR):
                        n = b * GR + g
                        e.wait_ge(oh_ready, GR * j + g + 1)
                        for k, ws in enumerate(BANKS):
                            need(e, win_out, WOUT * j + NBK * (g - 1) + k + 1)
                            for q, w in enumerate(ws):
                                for h in range(WT):
                                    t = (n % OR * OG + w) * WT + h
                                    ins = e.matmul(PS[:, k, q * KW:(q + 1) * KW], LOH[:, t, :], KOH[:, t, :], start=h == 0, stop=h == WT - 1)
                            ins.then_inc(win_ready, 1)
                    need(e, h0_taken, j - 1)
                    e.wait_ge(rows_in[b], 16 * BT * (i + 1))
                    for g in range(LR):
                        e.wait_ge(ow_ready, LR * j + g + 1)
                        for q in range(min(LG, BT - g * LG)):
                            t = g * LG + q
                            ins = e.matmul(PS[0:BN, 5 + b, 0:D], OHW[:, ((b * LR + g) % OR) * LG + q, :], G[:, b, t, :],
                                           start=t == 0, stop=t == BT - 1)
                        ins.then_inc(ow_used, 1)
                        e.wait_ge(win_out, WOUT * (j + 1))
                        for n in range(*TSPLIT[g:g + 2]):
                            need(e, tr_out, TROUT * j + n - 1)
                            settled(e)
                            bank = PS[:, 3 + (b * TROUT + n) % 2, :]
                            for k, h in enumerate(range(TB * n, min(TB * n + TB, NB))):
                                ins = e.matmul(bank[:, k * PITCH:(k + 1) * PITCH], slots[:, b, h * PITCH:(h + 1) * PITCH], ident_b[:, :],
                                               start=True, stop=True)
                            ins.then_inc(tr_ready, 1)

            build_turn(0)
            with e.Fori(0, NB // 2 - 1) as i:
                build_turn(i + 1)

            e.wait_ge(total_ready, 1)
            e.matmul(PS[0:1, 7, 0:1], total[:, 0:1], total[:, 1:2], start=True, stop=True).then_inc(total_sum, 1)
            e.wait_ge(slow_ready, 1)
            general = e.value_load(slow[0:1, 0:1], min_val=0, max_val=1)

            def general_sums(c):
                with e.Fori(0, NT) as t:
                    e.wait_ge(gz["msg"], NT * c + t + 1)
                    e.matmul(PS[:, 6, 0:HW], g_same[:, :], g_msg[:, :], start=True, stop=True).then_inc(gz["sum"], 1)

            with e.If(general > 0):
                general_sums(0)

            def parts(p):
                x3 = X_IN[p]
                wide = {0: XW, 1: HW, 2: 2 * D, 3: XW, 4: 2 * D}[p]
                f = F_OF.get(p)
                ts = 2 if p == 3 else 1
                turned = PS[:, 6 if p == 3 else 5, :]

                def turn_input(g, u):
                    j = RING * g + u
                    if p == 1:
                        e.wait_ge(row_ready, j + 1)
                    else:
                        e.wait_ge(agg_taken, NB * p + j + 1)
                    need(e, ts_ready, TS0[p] + ts * j)
                    if p == 4:
                        settled(e)
                        e.transpose(turned[0:D, 0:BN], MX[:, u, 0:D], ident_f[0:BN, 0:BN]).then_inc(mt_ready, 1)
                    else:
                        ins = e.transpose(turned[:, 0:BN], MX[:, u, :], ident_f[0:BN, 0:BN])
                        if p == 3:
                            ins = e.transpose(turned[0:D, P:P + BN], MO[:, u, :], ident_f[0:BN, 0:BN])
                        ins.then_inc(mt_ready, 1)

                def hidden(g, u):
                    j = RING * g + u
                    e.wait_ge(ts_ready, TS0[p] + j + 1)
                    need(e, h1_out, 2 * j)
                    for c in range(2):
                        ins = e.matmul(PS[:, 6, c * P:c * P + BN], W4a[:, c * P:(c + 1) * P], TS[0:D, 0, 0:BN], start=True, stop=True)
                    ins.then_inc(h1_ready, 1)

                def output(g, u):
                    j = RING * g + u
                    need(e, o_taken, NB * f + j)
                    o = PS[0:BN, 7, 0:D]
                    if p == 4:
                        e.wait_ge(h1_out, 2 * (j + 1))
                        e.matmul(o, H1[:, 0, :], W4b[:, 0, :], start=True, stop=False)
                        ins = e.matmul(o, H1[:, 1, :], W4b[:, 1, :], start=False, stop=True)
                    else:
                        e.wait_ge(ts_ready, TS0[p] + ts * (j + 1))
                        W = (W1, W2, None, W3)[p]
                        ins = e.matmul(o, TS[:, 0, 0:BN], W[:, :], start=True, stop=p != 3)
                        if p == 3:
                            ins = e.matmul(o, TS[0:D, 1, 0:BN], W3o[:, :], start=False, stop=True)
                    ins.then_inc(o_ready, 1)

                def ready(g, u):
                    e.wait_ge(slot_in[u], 16 * (NG * p + g + 1))
                    if p == 3:
                        if u == 0:
                            e.wait_ge(agg_taken, NB * p + (-2 if isinstance(g, int) and g == 0 else RING * (g - 1)))
                    else:
                        need(e, agg_taken, NB * p + RING * g + u - RING + 1)
                    settled(e)

                def products(u, a, b, fast, odd):
                    sums = group_sums(odd) if p == 3 else PS[:, 0:RING, :]
                    if not fast:
                        if b == NB:
                            e.matmul(sums[0:BN, u, 0:wide], ident_f[0:BN, 0:BN], GA[:, u, 0:wide], start=True, stop=True).then_inc(slot_used[u], 1)
                        return
                    for n in range(a, b):
                        if p == 3:
                            k, q = n // RING, n % RING
                            last = u == RING - 1 and k == NB // RING - 1
                            m = e.matmul(sums[:, q, 0:wide], slots[:, u, n * PITCH:(n + 1) * PITCH], x3[:, u * (NB // RING) + k, 0:wide],
                                         start=u == 0 and k == 0 and q % 2 == 0, stop=last and (q % 2 == 1 or q == RING - 1))
                        else:
                            m = e.matmul(sums[:, u, 0:wide], slots[:, u, n * PITCH:(n + 1) * PITCH], x3[:, n, 0:wide],
                                         start=n == 0, stop=n == NB - 1)
                    if b == NB:
                        m.then_inc(slot_used[u], 1)

                return turn_input, hidden, output, ready, products

            def turn(p, g, gather, fin, fast, odd=0):
                turn_input, hidden, output, ready, products = parts(p)
                if p == 3 and gather and fin:
                    for u in range(RING):
                        ready(g, u)
                        products(u, 0, NB // 2, fast, odd)
                        if u > 0:
                            turn_input(g - 1, u - 1)
                        products(u, NB // 2, NB, fast, odd)
                        if u > 0:
                            output(g - 1, u - 1)
                    turn_input(g - 1, RING - 1)
                    output(g - 1, RING - 1)
                    return
                for u in range(RING):
                    if fin:
                        turn_input(g - 1, u)
                    if gather:
                        ready(g, u)
                        products(u, 0, NB // 2, fast, odd)
                    if fin and p == 4:
                        hidden(g - 1, u)
                    if gather:
                        products(u, NB // 2, NB, fast, odd)
                    if fin:
                        output(g - 1, u)

            def change(p):
                EARLY = NB - RING - 1
                turn_input, _, output, _, _ = parts(p - 1)
                _, _, _, ready, products = parts(p)
                for u in range(RING):
                    turn_input(NG - 1, u)
                    ready(0, u)
                    for a, b in ((0, NB // 2), (NB // 2, EARLY)):
                        if u == 0:
                            e.wait_ge(x3_ready, X_NEED[p] - NB + b)
                        products(u, a, b, True, 0)
                    output(NG - 1, u)
                e.wait_ge(x3_ready, X_NEED[p])
                for u in range(RING):
                    products(u, EARLY, NB, True, 0)

            def turns(p, fast):
                after_output = p in (1, 2, 4)
                if fast and after_output:
                    change(p)
                else:
                    if after_output:
                        turn(p - 1, NG, False, True, fast)
                    e.wait_ge(x3_ready, X_NEED[p])
                    if not fast:
                        general_sums(p + 1)
                    turn(p, 0, True, False, fast)
                turn(p, 1, True, p != 2, fast, 1)
                if p == 3:
                    with e.Fori(0, NG // 2 - 1) as i:
                        turn(p, 2 * i + 2, True, True, fast, 0)
                        turn(p, 2 * i + 3, True, True, fast, 1)
                else:
                    with e.Fori(0, NG - 2) as i:
                        turn(p, i + 2, True, p != 2, fast)

            for p in range(5):
                with e.If(general > 0):
                    turns(p, False)
                with e.Else():
                    turns(p, True)
            turn(4, NG, False, True, True)


def kernel(**inputs):
    import concourse.bacc as bacc
    import numpy as np
    from concourse.bass_utils import run_bass_kernel_spmd

    v = {k: np.asarray(a) for k, a in inputs.items()}

    def nodes(a):
        return np.ascontiguousarray(a.reshape(NB, BN, -1).transpose(1, 0, 2))

    def padded(a, fill):
        return np.concatenate([a, np.full(EP - E, fill, a.dtype)])

    arrays = {
        "x_t": nodes(v["x"]),
        "cj_t": nodes(v["node_vec1"])[:, :, 0],
        "ci_t": nodes(v["node_vec1_n2"])[:, :, 0],
        "src_p": padded(v["src"], 0),
        "dst_p": padded(v["dst"], 2 * N),
        "samples": np.concatenate([v["dst"][::P], np.full(SCOLS * P - SAMP, P * BN, v["dst"].dtype)]).reshape(P, SCOLS),
        "edge_attr": v["edge_attr_64"],
        "ps_w": v["L0_gnn_ps_w"],
        "w1": np.concatenate([v["L1_gnn_W1_l"].T, v["L1_gnn_W1_r"].T]),
        "b1": v["L1_gnn_b1"],
        "w2": np.concatenate([v["L1_gnn_W2_l"].T, v["L1_gnn_W2_r"].T]),
        "b2": v["L1_gnn_b2"],
        "w3": np.concatenate([v["L2_gnn_W_s2d"], v["L2_gnn_W_self"]]),
        "w3o": v["L2_gnn_W_d2s"],
        "b3s": v["L2_gnn_b_self"],
        "b3i": v["L2_gnn_b_s2d"],
        "b3o": v["L2_gnn_b_d2s"],
        "w4a": v["L3_gnn_W1"],
        "b4a": v["L3_gnn_b1"],
        "w4b": v["L3_gnn_W2"],
        "b4b": v["L3_gnn_b2"],
        "eps": v["L3_gnn_eps"],
    }
    arrays = {k: np.ascontiguousarray(a) for k, a in arrays.items()}
    nc = bacc.Bacc("TRN2", target_bir_lowering=False, num_devices=1)
    args = [nc.dram_tensor(k, a.shape, mybir.dt.from_np(a.dtype), kind="ExternalInput").ap() for k, a in arrays.items()]
    args.append(nc.dram_tensor("out", (N, D), F32, kind="ExternalOutput").ap())
    build(nc, *args)
    return run_bass_kernel_spmd(nc, [arrays], core_ids=[0]).results[0]["out"]
```
